# Optimizing a Trainium2 kernel written in Bass

```python
import numpy as np
import jax
import jax.numpy as jnp

def _softmax(x, axis=-1):
    return jax.nn.softmax(x, axis=axis)

def _gelu(x):
    return jax.nn.gelu(x, approximate=True)

def _silu(x):
    return jax.nn.silu(x)

def _sigmoid(x):
    return jax.nn.sigmoid(x)

def _layernorm(x, axis=-1, eps=1e-05):
    m = jnp.mean(x, axis=axis, keepdims=True)
    v = jnp.var(x, axis=axis, keepdims=True)
    return (x - m) / jnp.sqrt(v + eps)

def _scatter_add(tgt, idx, src, axis=0):
    return tgt.at[idx].add(src)

def _segment_sum(src, seg, n):
    return jax.ops.segment_sum(src, seg, n)
kernel_name = 'mk_lm_tower_d1_tok_ids768_r4_317f6e'

def setup_inputs(seed: int=0):
    np.random.seed(seed)
    _w = jnp.asarray

    def _rec_inputs():
        import jax
        import jax.numpy as jnp
        _rk = jax.random.key(seed)
        x = jax.random.randint(jax.random.fold_in(_rk, 1), (16, 128), 0, 30522, jnp.int32)
        mask_BS_i1_0 = jnp.where(jnp.ones((16, 128), dtype=bool), 1, 0).astype(jnp.int32)
        return (x, mask_BS_i1_0)
    x, mask_BS_i1_0 = _rec_inputs()

    def _L0_tok_setup():
        import jax, jax.numpy as jnp
        import numpy as np
        VOCAB = 30522
        SEG_VOCAB = 2
        D_MODEL = 192
        MAX_LEN = 128
        B, S = (64, 128)
        EPS = 1e-05
        key = jax.random.key(seed)
        k1, k2, k3, k4, k5 = jax.random.split(key, 5)
        token_ids = jax.random.randint(k1, (B, S), 0, VOCAB)
        segment_ids = jax.random.randint(k2, (B, S), 0, SEG_VOCAB)
        tok_table = jax.random.normal(k3, (VOCAB, D_MODEL), dtype=jnp.float32) * 0.02
        seg_table = jax.random.normal(k4, (SEG_VOCAB, D_MODEL), dtype=jnp.float32) * 0.02
        pos_table = jax.random.normal(k5, (MAX_LEN, D_MODEL), dtype=jnp.float32) * 0.02
        gamma = jnp.ones((D_MODEL,), dtype=jnp.float32)
        beta = jnp.zeros((D_MODEL,), dtype=jnp.float32)
        return {'token_ids': token_ids, 'segment_ids': segment_ids, 'tok_table': tok_table, 'seg_table': seg_table, 'pos_table': pos_table, 'gamma': gamma, 'beta': beta}
    _L0_tok_all = _L0_tok_setup()
    _L0_tok_in = {k: v for k, v in _L0_tok_all.items() if k in ('tok_table', 'seg_table', 'pos_table', 'gamma', 'beta')}
    del _L0_tok_all

    def _L0_attn_setup():
        import jax, jax.numpy as jnp
        import numpy as np
        import math
        D_MODEL = 192
        N_HEADS = 6
        HD = D_MODEL // N_HEADS
        RANK = D_MODEL // 4
        B, T = (128, 64)

        def _rope_tables(T, dim):
            inv = 1.0 / 10000.0 ** (jnp.arange(0, dim, 2, dtype=jnp.float32) / dim)
            t = jnp.arange(T, dtype=jnp.float32)
            freqs = jnp.outer(t, inv)
            emb = jnp.concatenate([freqs, freqs], axis=-1)
            return (jnp.cos(emb), jnp.sin(emb))

        def _rot(x):
            h = x.shape[-1] // 2
            return jnp.concatenate([-x[..., h:], x[..., :h]], axis=-1)
        key = jax.random.key(seed)
        ks = jax.random.split(key, 8)
        s_in = 1.0 / math.sqrt(D_MODEL)
        s_r = 1.0 / math.sqrt(RANK)
        inp = {'x': jax.random.normal(ks[0], (B, T, D_MODEL), dtype=jnp.float32), 'qA': jax.random.normal(ks[1], (D_MODEL, RANK), dtype=jnp.float32) * s_in, 'qB': jax.random.normal(ks[2], (RANK, D_MODEL), dtype=jnp.float32) * s_r, 'kA': jax.random.normal(ks[3], (D_MODEL, RANK), dtype=jnp.float32) * s_in, 'kB': jax.random.normal(ks[4], (RANK, D_MODEL), dtype=jnp.float32) * s_r, 'vA': jax.random.normal(ks[5], (D_MODEL, RANK), dtype=jnp.float32) * s_in, 'vB': jax.random.normal(ks[6], (RANK, D_MODEL), dtype=jnp.float32) * s_r, 'o_w': jax.random.normal(ks[7], (D_MODEL, D_MODEL), dtype=jnp.float32) * s_in}
        return inp
    _L0_attn_all = _L0_attn_setup()
    _L0_attn_in = {k: v for k, v in _L0_attn_all.items() if k in ('qA', 'qB', 'kA', 'kB', 'vA', 'vB', 'o_w')}
    del _L0_attn_all

    def _L0_ffn_setup():
        import math
        import jax, jax.numpy as jnp
        import numpy as np
        EMBED_CHOICES = [96, 144, 192]
        RATIO_CHOICES = [2, 3, 4]
        E_MAX = 192
        H_MAX = 768

        def new_gelu(x):
            c = math.sqrt(2.0 / math.pi)
            return 0.5 * x * (1.0 + jnp.tanh(c * (x + 0.044715 * x * x * x)))

        def _mixed_coeffs(alpha_e, alpha_r):
            h_idx = jnp.arange(H_MAX)
            d_idx = jnp.arange(E_MAX)
            C0 = jnp.zeros((H_MAX, E_MAX), jnp.float32)
            c0b = jnp.zeros((H_MAX,), jnp.float32)
            C1 = jnp.zeros((E_MAX, H_MAX), jnp.float32)
            c1b = jnp.zeros((E_MAX,), jnp.float32)
            for i, e in enumerate(EMBED_CHOICES):
                m_in = (d_idx < e).astype(jnp.float32)
                for j, r in enumerate(RATIO_CHOICES):
                    a = alpha_e[i] * alpha_r[j]
                    m_out = (h_idx < r * e).astype(jnp.float32)
                    C0 = C0 + a * (m_out[:, None] * m_in[None, :])
                    c0b = c0b + a * m_out
                    C1 = C1 + a * (m_in[:, None] * m_out[None, :])
                    c1b = c1b + a * m_in
            return (C0, c0b, C1, c1b)
        key = jax.random.key(seed)
        ks = jax.random.split(key, 6)
        x = jax.random.normal(ks[0], (8, 512, E_MAX), jnp.float32)
        w_fc = jax.random.normal(ks[1], (H_MAX, E_MAX), jnp.float32) * 0.02
        b_fc = jnp.zeros((H_MAX,), jnp.float32)
        w_proj = jax.random.normal(ks[2], (E_MAX, H_MAX), jnp.float32) * 0.02
        b_proj = jnp.zeros((E_MAX,), jnp.float32)
        alpha_e = jax.nn.softmax(jax.random.normal(ks[3], (3,), jnp.float32))
        alpha_r = jax.nn.softmax(jax.random.normal(ks[4], (3,), jnp.float32))
        return {'x': x, 'w_fc': w_fc, 'b_fc': b_fc, 'w_proj': w_proj, 'b_proj': b_proj, 'alpha_e': alpha_e, 'alpha_r': alpha_r}
    _L0_ffn_all = _L0_ffn_setup()
    _L0_ffn_in = {k: v for k, v in _L0_ffn_all.items() if k in ('w_fc', 'b_fc', 'w_proj', 'b_proj', 'alpha_e', 'alpha_r')}
    del _L0_ffn_all
    return {'x': x, 'mask_BS_i1_0': mask_BS_i1_0, 'L0_tok_tok_table': _L0_tok_in['tok_table'], 'L0_tok_seg_table': _L0_tok_in['seg_table'], 'L0_tok_pos_table': _L0_tok_in['pos_table'], 'L0_tok_gamma': _L0_tok_in['gamma'], 'L0_tok_beta': _L0_tok_in['beta'], 'L0_attn_qA': _L0_attn_in['qA'], 'L0_attn_qB': _L0_attn_in['qB'], 'L0_attn_kA': _L0_attn_in['kA'], 'L0_attn_kB': _L0_attn_in['kB'], 'L0_attn_vA': _L0_attn_in['vA'], 'L0_attn_vB': _L0_attn_in['vB'], 'L0_attn_o_w': _L0_attn_in['o_w'], 'L0_ffn_w_fc': _L0_ffn_in['w_fc'], 'L0_ffn_b_fc': _L0_ffn_in['b_fc'], 'L0_ffn_w_proj': _L0_ffn_in['w_proj'], 'L0_ffn_b_proj': _L0_ffn_in['b_proj'], 'L0_ffn_alpha_e': _L0_ffn_in['alpha_e'], 'L0_ffn_alpha_r': _L0_ffn_in['alpha_r']}

def reference(x, mask_BS_i1_0, L0_tok_tok_table, L0_tok_seg_table, L0_tok_pos_table, L0_tok_gamma, L0_tok_beta, L0_attn_qA, L0_attn_qB, L0_attn_kA, L0_attn_kB, L0_attn_vA, L0_attn_vB, L0_attn_o_w, L0_ffn_w_fc, L0_ffn_b_fc, L0_ffn_w_proj, L0_ffn_b_proj, L0_ffn_alpha_e, L0_ffn_alpha_r):
    import jax
    import jax.numpy as jnp

    def _L0_tok_ref(token_ids, segment_ids, tok_table, seg_table, pos_table, gamma, beta):
        import jax, jax.numpy as jnp
        import numpy as np
        VOCAB = 30522
        SEG_VOCAB = 2
        D_MODEL = 192
        MAX_LEN = 128
        B, S = (64, 128)
        EPS = 1e-05
        seq_len = token_ids.shape[1]
        emb = tok_table[token_ids] + seg_table[segment_ids] + pos_table[:seq_len][None, :, :]
        mu = jnp.mean(emb, axis=-1, keepdims=True)
        var = jnp.mean(jnp.square(emb - mu), axis=-1, keepdims=True)
        out = (emb - mu) * jax.lax.rsqrt(var + EPS) * gamma + beta
        return out

    def _L0_attn_ref(x, qA, qB, kA, kB, vA, vB, o_w):
        import jax, jax.numpy as jnp
        import numpy as np
        import math
        D_MODEL = 192
        N_HEADS = 6
        HD = D_MODEL // N_HEADS
        RANK = D_MODEL // 4
        B, T = (128, 64)

        def _rope_tables(T, dim):
            inv = 1.0 / 10000.0 ** (jnp.arange(0, dim, 2, dtype=jnp.float32) / dim)
            t = jnp.arange(T, dtype=jnp.float32)
            freqs = jnp.outer(t, inv)
            emb = jnp.concatenate([freqs, freqs], axis=-1)
            return (jnp.cos(emb), jnp.sin(emb))

        def _rot(x):
            h = x.shape[-1] // 2
            return jnp.concatenate([-x[..., h:], x[..., :h]], axis=-1)
        Bb, Tt, _ = x.shape

        def proj(A, W):
            h = x @ A @ W
            return h.reshape(Bb, Tt, N_HEADS, HD).transpose(0, 2, 1, 3)
        q = proj(qA, qB)
        k = proj(kA, kB)
        v = proj(vA, vB)
        cos, sin = _rope_tables(Tt, HD)
        q = q * cos + _rot(q) * sin
        k = k * cos + _rot(k) * sin
        att = jnp.einsum('bhqd,bhkd->bhqk', q, k) / math.sqrt(HD)
        causal = jnp.tril(jnp.ones((Tt, Tt), dtype=bool))
        att = jnp.where(causal, att, -jnp.inf)
        att = jax.nn.softmax(att, axis=-1)
        out = jnp.einsum('bhqk,bhkd->bhqd', att, v)
        out = out.transpose(0, 2, 1, 3).reshape(Bb, Tt, D_MODEL)
        return out @ o_w

    def _L0_ffn_ref(x, w_fc, b_fc, w_proj, b_proj, alpha_e, alpha_r):
        import math
        import jax, jax.numpy as jnp
        import numpy as np
        EMBED_CHOICES = [96, 144, 192]
        RATIO_CHOICES = [2, 3, 4]
        E_MAX = 192
        H_MAX = 768

        def new_gelu(x):
            c = math.sqrt(2.0 / math.pi)
            return 0.5 * x * (1.0 + jnp.tanh(c * (x + 0.044715 * x * x * x)))

        def _mixed_coeffs(alpha_e, alpha_r):
            h_idx = jnp.arange(H_MAX)
            d_idx = jnp.arange(E_MAX)
            C0 = jnp.zeros((H_MAX, E_MAX), jnp.float32)
            c0b = jnp.zeros((H_MAX,), jnp.float32)
            C1 = jnp.zeros((E_MAX, H_MAX), jnp.float32)
            c1b = jnp.zeros((E_MAX,), jnp.float32)
            for i, e in enumerate(EMBED_CHOICES):
                m_in = (d_idx < e).astype(jnp.float32)
                for j, r in enumerate(RATIO_CHOICES):
                    a = alpha_e[i] * alpha_r[j]
                    m_out = (h_idx < r * e).astype(jnp.float32)
                    C0 = C0 + a * (m_out[:, None] * m_in[None, :])
                    c0b = c0b + a * m_out
                    C1 = C1 + a * (m_in[:, None] * m_out[None, :])
                    c1b = c1b + a * m_in
            return (C0, c0b, C1, c1b)
        C0, c0b, C1, c1b = _mixed_coeffs(alpha_e, alpha_r)
        W0 = w_fc * C0
        b0 = b_fc * c0b
        h = jnp.einsum('bte,he->bth', x, W0) + b0
        h = new_gelu(h)
        W1 = w_proj * C1
        b1 = b_proj * c1b
        out = jnp.einsum('bth,eh->bte', h, W1) + b1
        return out
    h = _L0_tok_ref(x, mask_BS_i1_0, L0_tok_tok_table, L0_tok_seg_table, L0_tok_pos_table, L0_tok_gamma, L0_tok_beta)
    h = h + _L0_attn_ref(_layernorm(h, axis=-1), L0_attn_qA, L0_attn_qB, L0_attn_kA, L0_attn_kB, L0_attn_vA, L0_attn_vB, L0_attn_o_w)
    h = h + _L0_ffn_ref(_layernorm(h, axis=-1), L0_ffn_w_fc, L0_ffn_b_fc, L0_ffn_w_proj, L0_ffn_b_proj, L0_ffn_alpha_e, L0_ffn_alpha_r)
    return h

_drawn_inputs = setup_inputs


def setup_inputs(seed=0):
    import zlib

    import numpy as np

    out = dict(_drawn_inputs(seed))
    spreads = {'L0_tok_gamma': (1.0, 0.2),
     'L0_tok_beta': (0.0, 0.1),
     'L0_ffn_b_fc': (0.0, 0.491),
     'L0_ffn_b_proj': (0.0, 0.1)}
    factors = {'L0_ffn_alpha_r': 5.557}
    for name, (base, spread) in spreads.items():
        noise = np.random.default_rng([zlib.crc32(name.encode()), seed]).standard_normal(out[name].shape)
        drawn = base * np.exp(spread * noise) if base else spread * noise
        out[name] = jnp.asarray(drawn.astype(out[name].dtype))
    for name, factor in factors.items():
        out[name] = (out[name] * factor).astype(out[name].dtype)
    return out
```

```python
import concourse.bass as bass
from concourse import mybir
from contextlib import ExitStack

B, T, D = 16, 128, 192
HEADS, HD = 6, 32
RANK = 48
HID = 768
KH = D // 2
HPB = HEADS // 2
PB = 512
VW = HD + 1
GROUP = 4
NG = B // GROUP
GT = GROUP * T
HC = HID // 128
EPS = 1e-5
MASKED = -1e30
SCALE = float(HD) ** -0.5
EMBEDS, RATIOS = (96, 144, 192), (2, 3, 4)
NC9 = len(EMBEDS) * len(RATIOS)

LAG_S, LAG_PV, LAG_OW = 1, 2, 3
LEAD_EMB, LEAD_LN0, LEAD_LN1 = 3, 2, 1
FIRST, LAST = -LEAD_EMB, B - 1 + LAG_OW
COEF_STEPS = {0: range(0, 3), 1: range(3, 7), 2: range(7, 4 + HC + 1)}
AHEAD = 3
STEADY = (LAG_OW + 1, B - LEAD_EMB)


def lm_layer(nc, ids, seg, tok_table, seg_table, pos_table, gamma, beta, qkvA, qkvB, o_w,
             w_fc, b_fc, w_proj, b_proj, alpha_e, alpha_r, m_in, m_out, rope_cos, rope_sin, out):
    fp32, bf16 = mybir.dt.float32, mybir.dt.bfloat16
    ALU, ACT, AX = mybir.AluOpType, mybir.ActivationFunctionType, mybir.AxisListType
    ctx = ExitStack()
    with ctx:
        def sb(name, shape, dt=fp32):
            return ctx.enter_context(nc.sbuf_tensor(name, shape, dt))

        def sem(name):
            return ctx.enter_context(nc.semaphore(name))

        ids_sb = sb("ids_sb", [T, B], mybir.dt.int32)
        seg_i = sb("seg_i", [T, B], mybir.dt.int32)
        seg_f = sb("seg_f", [T, B])
        seg_rows = sb("seg_rows", [T, 2 * D])
        seg_diff = sb("seg_diff", [T, D])
        pos_sb = sb("pos_sb", [T, D])
        gamma_sb = sb("gamma_sb", [T, D])
        beta_sb = sb("beta_sb", [T, D])
        projA = sb("projA", [RANK, 3 * D])
        projB = sb("projB", [RANK, 3 * D])
        wqkv = sb("wqkv", [KH, 2 * 3 * D])
        wo_sb = sb("wo_sb", [KH, 2 * D])
        fc_raw = sb("fc_raw", [KH, 2 * HID])
        w0 = sb("w0", [KH, 2 * HID])
        proj_raw = sb("proj_raw", [128, HC * D])
        w1 = sb("w1", [128, HC * D])
        bfc_sb = sb("bfc_sb", [128, HC])
        b0 = sb("b0", [128, HC])
        bproj_sb = sb("bproj_sb", [T, D])
        b1 = sb("b1", [T, D])
        alphas = sb("alphas", [NC9, 2])
        m_in_sb = sb("m_in_sb", [NC9, D])
        m_out_sb = sb("m_out_sb", [NC9, HID])
        mix = sb("mix", [NC9, D + 1])
        ones9 = sb("ones9", [NC9, T])
        cos_sb = sb("cos_sb", [T, HD])
        sin_sb = sb("sin_sb", [T, HD])
        ident = sb("ident", [128, 128])
        ident_b = sb("ident_b", [128, 128], bf16)
        causal = sb("causal", [128, T], bf16)
        half_neg = sb("half_neg", [T, 1])
        eps_sb = sb("eps_sb", [T, 1])

        H = sb("H", [T, B * D])
        seg_add = sb("seg_add", [T, D])
        emb_sum = sb("emb_sum", [T, D])
        bn = [sb(f"bn{k}", [T, 6]) for k in range(3)]
        mv = [sb(f"mv{k}", [T, 2]) for k in range(3)]
        ve = [sb(f"ve{k}", [T, 1]) for k in range(3)]
        rstd = [sb(f"rstd{k}", [T, 1]) for k in range(3)]
        x1 = sb("x1", [T, D])
        x1T = sb("x1T", [KH, 2 * T])
        cos_part = sb("cos_part", [T, 2 * D])
        sin_part = sb("sin_part", [T, 2 * D])
        qk = sb("qk", [T, 2 * D])
        qkT = sb("qkT", [KH, 4 * T])
        vaug = sb("vaug", [T, B * HEADS * VW])
        smax = sb("smax", [T, HEADS])
        nmax = sb("nmax", [T, HEADS])
        p = sb("p", [T, HEADS * T])
        pT = sb("pT", [T, HEADS * T])
        rsum = sb("rsum", [T, HEADS])
        o = sb("o", [T, D])
        oT = sb("oT", [KH, 2 * T])
        x2 = sb("x2", [T, D])
        x2T = sb("x2T", [KH, 2 * B * T])
        hT = sb("hT", [128, HC * GT])

        def pb(name, banks=1):
            return ctx.enter_context(nc.psum_tensor(name, [128, banks * PB], fp32))

        ps_qk, ps_v, ps_pv, ps_ow, ps_x = (pb(f"ps_{n}")[:, :] for n in ("qk", "v", "pv", "ow", "x"))
        ps_s = pb("ps_s", HPB)
        s_bank = [ps_s[:, j * PB:(j + 1) * PB] for j in range(HPB)]
        s_all = ps_s[:, :].rearrange("p (j n) -> p j n", j=HPB)[:, :, 0:2 * T]
        ps_w = [ps_qk, ps_v, *s_bank, ps_pv]
        ps_c = [ps_ow, ps_x]
        ps_h = [ps_x, *s_bank[:2]]
        ps_y = [ps_qk, ps_v, ps_pv, ps_ow]

        ids_in = sem("ids_in")
        emb_in = sem("emb_in")
        attn_in = sem("attn_in")
        rope_in = sem("rope_in")
        ffn_in = sem("ffn_in")
        tok_in = [sem(f"tok_in{b}") for b in range(B)]
        tok_rows = sem("tok_rows")
        pool_c = sem("pool_c")
        consts_done = sem("consts_done")
        seg_done = sem("seg_done")
        wqkv_ps = sem("wqkv_ps")
        wqkv_done = sem("wqkv_done")
        mix_done = sem("mix_done")
        coef_ps = sem("coef_ps")
        coef_used = sem("coef_used")
        emb_done = sem("emb_done")
        stats = [sem(f"stats{k}") for k in range(3)]
        rstd_done = [sem(f"rstd_done{k}") for k in range(3)]
        ve_done = [sem(f"ve_done{k}") for k in range(3)]
        bn_done = [sem(f"bn_done{k}") for k in range(3)]
        seg_added = sem("seg_added")
        emb_summed = sem("emb_summed")
        scaled = sem("scaled")
        h1_done = sem("h1_done")
        rope_parts = sem("rope_parts")
        smax_done = sem("smax_done")
        rsum_done = sem("rsum_done")
        norm0_done = sem("norm0_done")
        h0_done = sem("h0_done")
        x1_done = sem("x1_done")
        x1T_ps = sem("x1T_ps")
        x1T_done = sem("x1T_done")
        qk_ps = sem("qk_ps")
        v_ps = sem("v_ps")
        v_done = sem("v_done")
        qk_done = sem("qk_done")
        qkT_ps = sem("qkT_ps")
        qkT_done = sem("qkT_done")
        s_ps = sem("s_ps")
        max_done = sem("max_done")
        p_done = sem("p_done")
        pT_ps = sem("pT_ps")
        pT_done = sem("pT_done")
        pv_ps = sem("pv_ps")
        o_done = sem("o_done")
        oT_ps = sem("oT_ps")
        oT_done = sem("oT_done")
        ow_ps = sem("ow_ps")
        x2_done = sem("x2_done")
        x2T_ps = sem("x2T_ps")
        x2T_done = sem("x2T_done")
        res_done = sem("res_done")
        h_ps = sem("h_ps")
        h_done = sem("h_done")
        h_used = sem("h_used")
        y_done = sem("y_done")
        stored = sem("stored")

        block = ctx.enter_context(nc.Block())

        def row(t, b):
            return t[:, bass.ts(b, D)]

        def pipeline(eng, step, after=None):
            for t in range(FIRST, STEADY[0]):
                step(t)
                if after:
                    after(t)
            with eng.Fori(STEADY[0], STEADY[1]) as t:
                step(t)
            for t in range(STEADY[1], LAST + 1):
                step(t)

        def wait_apart(eng, sem, count):
            if not isinstance(count, int):
                eng.wait_ge(sem, 1)
            eng.wait_ge(sem, count)

        def is_row(t, d):
            return not isinstance(t, int) or 0 <= t - d < B

        def later(t, d=0):
            return not isinstance(t, int) or t - d >= 1

        @block.sync
        def _(sp):
            sp.dma_start(ids_sb[:, :], ids).then_inc(ids_in, 16)
            sp.dma_start(seg_i[:, :], seg).then_inc(emb_in, 16)
            sp.dma_start(seg_rows[:, :], seg_table.partition_broadcast(T)).then_inc(emb_in, 16)
            sp.dma_start(pos_sb[:, :], pos_table).then_inc(emb_in, 16)
            sp.dma_start(gamma_sb[:, :], gamma.partition_broadcast(T)).then_inc(emb_in, 16)
            sp.dma_start(beta_sb[:, :], beta.partition_broadcast(T)).then_inc(emb_in, 16)
            sp.dma_start(cos_sb[:, :], rope_cos).then_inc(rope_in, 16)
            sp.dma_start(sin_sb[:, :], rope_sin).then_inc(rope_in, 16)
            for b in range(B):
                sp.wait_ge(tok_in[b], 16)
                sp.sem_inc(tok_rows, 1)
            with sp.Fori(0, NG) as g:
                sp.wait_ge(y_done, g * GROUP + GROUP)
                sp.dma_start(out[bass.ts(g, GROUP), :, :].rearrange("b t d -> t b d"),
                             H[:, bass.ts(g, GROUP * D)].rearrange("t (b d) -> t b d", d=D))\
                  .then_inc(stored, 16)
            sp.wait_ge(stored, 16 * NG)

        @block.gpsimd
        def _(pool):
            pool.wait_ge(ids_in, 16)

            def gather(b):
                pool.indirect_dma_start(out=row(H, b), out_offset=None, in_=tok_table,
                                        in_offset=bass.IndirectOffsetOnAxis(ap=ids_sb[:, b:b + 1], axis=0))\
                    .then_inc(tok_in[b], 16)

            for b in range(AHEAD):
                gather(b)
            pool.memset(ident[:, :], 0.0).then_inc(pool_c, 1)
            pool.memset(ident_b[:, :], 0.0).then_inc(pool_c, 1)
            pool.memset(causal[:, :], 0.0).then_inc(pool_c, 1)
            pool.memset(vaug[:, :], 1.0).then_inc(pool_c, 1)
            pool.memset(half_neg[:, :], -0.5).then_inc(pool_c, 1)
            pool.memset(eps_sb[:, :], EPS).then_inc(pool_c, 1)
            pool.memset(ones9[:, :], 1.0).then_inc(pool_c, 1)
            pool.wait_ge(pool_c, 7)
            for m in (ident, ident_b):
                pool.affine_select(out=m[:, :], in_=m[:, :], compare_op=ALU.not_equal, fill=1.0, base=0,
                                   pattern=[[-1, 128]], channel_multiplier=1).then_inc(consts_done, 1)
            pool.affine_select(out=causal[:, :], in_=causal[:, :], compare_op=ALU.is_ge, fill=MASKED, base=0,
                               pattern=[[-1, T]], channel_multiplier=1).then_inc(consts_done, 1)
            pool.wait_ge(seg_done, 3)

            def inv_std(k, b):
                wait_apart(pool, stats[k], b + 1)
                pool.tensor_tensor(ve[k][:, :], mv[k][:, 1:2], eps_sb[:, :], ALU.add).then_inc(ve_done[k], 1)
                pool.wait_ge(ve_done[k], b + 1)
                pool.tensor_tensor(rstd[k][:, :], ve[k][:, :], half_neg[:, :], ALU.pow)\
                    .then_inc(rstd_done[k], 1)

            def step(t):
                if is_row(t, -LEAD_LN0):
                    b = t + LEAD_LN0
                    wait_apart(pool, norm0_done, b + 1)
                    pool.tensor_tensor(row(H, b), row(H, b), gamma_sb[:, :], ALU.mult).then_inc(scaled, 1)
                    wait_apart(pool, scaled, b + 1)
                    pool.tensor_tensor(row(H, b), row(H, b), beta_sb[:, :], ALU.add).then_inc(h0_done, 1)
                if is_row(t, LAG_OW):
                    inv_std(2, t - LAG_OW)
                if is_row(t, -LEAD_EMB):
                    b = t + LEAD_EMB
                    pool.tensor_tensor(seg_add[:, :], seg_diff[:, :],
                                       seg_f[:, bass.ds(b, 1)].to_broadcast([T, D]), ALU.mult)\
                        .then_inc(seg_added, 1)
                    wait_apart(pool, seg_added, b + 1)
                    pool.tensor_tensor(emb_sum[:, :], seg_add[:, :], pos_sb[:, :], ALU.add)\
                        .then_inc(emb_summed, 1)
                    wait_apart(pool, emb_summed, b + 1)
                    pool.wait_ge(tok_rows, b + 1)
                    pool.tensor_tensor(row(H, b), row(H, b), emb_sum[:, :], ALU.add).then_inc(emb_done, 1)
                if is_row(t, -LEAD_LN0):
                    inv_std(1, t + LEAD_LN0)
                if is_row(t, -LEAD_EMB):
                    inv_std(0, t + LEAD_EMB)

            def more_rows(t):
                for b in range(AHEAD + (t - FIRST) * 2, min(AHEAD + (t - FIRST) * 2 + 2, B)):
                    gather(b)

            pipeline(pool, step, more_rows)

            with pool.Fori(0, NG) as g:
                wait_apart(pool, x2_done, g * GROUP + GROUP)
                rows = H[:, bass.ts(g, GROUP * D)].rearrange("t (b d) -> t b d", d=D)
                pool.tensor_tensor(rows, rows, b1[:, :].unsqueeze(1).to_broadcast([T, GROUP, D]), ALU.add)\
                    .then_inc(res_done, 1)

        @block.scalar
        def _(act):
            act.dma_start(projA[:, :], qkvA).then_inc(attn_in, 16)
            act.dma_start(projB[:, :], qkvB).then_inc(attn_in, 16)
            act.dma_start(wo_sb[:, :].rearrange("p (c n) -> p c n", c=2),
                          o_w.rearrange("(c p) n -> p c n", p=KH)).then_inc(attn_in, 16)
            act.dma_start(alphas[:, 0:1], alpha_e).then_inc(ffn_in, 16)
            act.dma_start(alphas[:, 1:2], alpha_r).then_inc(ffn_in, 16)
            act.dma_start(m_in_sb[:, :], m_in).then_inc(ffn_in, 16)
            act.dma_start(m_out_sb[:, :], m_out).then_inc(ffn_in, 16)
            act.dma_start(fc_raw[:, :].rearrange("p (c n) -> p c n", c=2),
                          w_fc.rearrange("(c p) n -> p c n", p=KH)).then_inc(ffn_in, 16)
            act.dma_start(proj_raw[:, :].rearrange("p (c n) -> p c n", c=HC),
                          w_proj.rearrange("(c p) n -> p c n", p=128)).then_inc(ffn_in, 16)
            act.dma_start(bfc_sb[:, :], b_fc).then_inc(ffn_in, 16)
            act.dma_start(bproj_sb[:, :], b_proj.partition_broadcast(T)).then_inc(ffn_in, 16)
            for n in range(6):
                act.wait_ge(wqkv_ps, n + 1)
                c, j = n % 2, n // 2
                act.copy(wqkv[:, c * 3 * D + j * D:c * 3 * D + (j + 1) * D], ps_w[n][0:KH, 0:D])\
                   .then_inc(wqkv_done, 1)

            def step(t):
                if is_row(t, LAG_PV):
                    b = t - LAG_PV
                    act.wait_ge(pT_ps, b + 1)
                    if later(t, LAG_PV):
                        act.wait_ge(pv_ps, b)
                    act.copy(pT[:, :].rearrange("p (j n) -> p j n", j=HPB), s_all).then_inc(pT_done, 1)
                if is_row(t, LAG_OW):
                    b = t - LAG_OW
                    act.wait_ge(oT_ps, b + 1)
                    if later(t, LAG_OW):
                        act.wait_ge(ow_ps, b)
                    act.copy(oT[:, :], ps_pv[0:KH, 0:2 * T]).then_inc(oT_done, 1)
                if is_row(t, LAG_S):
                    b = t - LAG_S
                    act.wait_ge(qkT_ps, b + 1)
                    if later(t, LAG_S):
                        act.wait_ge(s_ps, b)
                    act.copy(qkT[:, :], ps_qk[0:KH, 0:4 * T]).then_inc(qkT_done, 1)
                if is_row(t, 0):
                    b = t
                    act.wait_ge(x1T_ps, b + 1)
                    if later(t, 0):
                        act.wait_ge(v_ps, b)
                    act.copy(x1T[:, :], ps_v[0:KH, 0:2 * T]).then_inc(x1T_done, 1)
                if is_row(t, LAG_S):
                    b = t - LAG_S
                    act.wait_ge(max_done, b + 1)
                    if later(t, LAG_S):
                        act.wait_ge(pT_ps, b)
                    for h in range(HEADS):
                        e = act.activation(p[:, h * T:(h + 1) * T],
                                           s_bank[h // 2][:, (h % 2) * T:(h % 2 + 1) * T],
                                           ACT.Exp, bias=nmax[:, h:h + 1], scale=SCALE)
                    e.then_inc(p_done, 1)
                if is_row(t, 0):
                    b = t
                    act.wait_ge(v_ps, b + 1)
                    act.copy(vaug[:, bass.ts(b, HEADS * VW)].rearrange("p (h e) -> p h e", e=VW)[:, :, 0:HD],
                             ps_v[:, 0:D].rearrange("p (h e) -> p h e", e=HD)).then_inc(v_done, 1)
                if is_row(t, LAG_OW):
                    b = t - LAG_OW
                    act.wait_ge(x2T_ps, b + 1)
                    act.copy(x2T[:, :].rearrange("p (c n) -> p c n", c=2)[:, :, bass.ts(b, T)],
                             ps_ow[0:KH, 0:2 * T].rearrange("p (c n) -> p c n", c=2)).then_inc(x2T_done, 1)

            pipeline(act, step)

            def gelu(g, m):
                act.wait_ge(h_ps, g * HC + m + 1)
                if later(g, 0):
                    act.wait_ge(h_used, (g - 1) * HC + m + 1)
                act.activation(hT[:, m * GT:(m + 1) * GT], ps_h[m % 3][:, :], ACT.Gelu_apprx_tanh,
                               bias=b0[:, m:m + 1]).then_inc(h_done, 1)

            for m in range(HC):
                gelu(0, m)
            with act.Fori(1, NG) as g:
                for m in range(HC):
                    gelu(g, m)

        @block.vector
        def _(dve):
            dve.wait_ge(emb_in, 5 * 16)
            dve.tensor_copy(seg_f[:, :], seg_i[:, :]).then_inc(seg_done, 1)
            dve.tensor_tensor(pos_sb[:, :], pos_sb[:, :], seg_rows[:, 0:D], ALU.add).then_inc(seg_done, 1)
            dve.tensor_tensor(seg_diff[:, :], seg_rows[:, D:2 * D], seg_rows[:, 0:D], ALU.subtract)\
               .then_inc(seg_done, 1)
            dve.wait_ge(rope_in, 2 * 16)

            def layer_stats(k, b, x):
                dve.bn_stats(bn[k][:, :], x).then_inc(bn_done[k], 1)
                wait_apart(dve, bn_done[k], b + 1)
                dve.bn_aggr(mv[k][:, :], bn[k][:, :]).then_inc(stats[k], 1)

            def normalize(k, b, dst, x, done):
                dve.wait_ge(rstd_done[k], b + 1)
                dve.tensor_scalar(dst, x, mv[k][:, 0:1], rstd[k][:, 0:1], ALU.subtract, ALU.mult)\
                   .then_inc(done, 1)

            def step(t):
                if is_row(t, -LEAD_LN0):
                    b = t + LEAD_LN0
                    normalize(0, b, row(H, b), row(H, b), norm0_done)
                if is_row(t, -LEAD_LN1):
                    b = t + LEAD_LN1
                    if later(t, -LEAD_LN1):
                        dve.wait_ge(x1T_ps, b)
                    normalize(1, b, x1[:, :], row(H, b), x1_done)
                if is_row(t, LAG_OW):
                    b = t - LAG_OW
                    dve.wait_ge(ow_ps, b + 1)
                    dve.tensor_tensor(row(H, b), row(H, b), ps_ow[:, 0:D], ALU.add).then_inc(h1_done, 1)
                    wait_apart(dve, h1_done, b + 1)
                    if later(t, LAG_OW):
                        dve.wait_ge(x2_done, b)
                    layer_stats(2, b, row(H, b))
                if is_row(t, LAG_S):
                    b = t - LAG_S
                    dve.wait_ge(s_ps, b + 1)
                    dve.tensor_reduce(smax[:, :].rearrange("p (j c) -> p j c", c=2),
                                      s_all.rearrange("p j (c k) -> p j c k", k=T), AX.X, ALU.max)\
                       .then_inc(smax_done, 1)
                    dve.wait_ge(smax_done, b + 1)
                    if later(t, LAG_S):
                        dve.wait_ge(p_done, b)
                    dve.tensor_scalar(nmax[:, :], smax[:, :], -SCALE, None, ALU.mult).then_inc(max_done, 1)
                if is_row(t, -LEAD_LN0):
                    b = t + LEAD_LN0
                    wait_apart(dve, h0_done, b + 1)
                    if later(t, -LEAD_LN0):
                        dve.wait_ge(x1_done, b)
                    layer_stats(1, b, row(H, b))
                if is_row(t, LAG_OW):
                    b = t - LAG_OW
                    if later(t, LAG_OW):
                        dve.wait_ge(x2T_ps, b)
                    normalize(2, b, x2[:, :], row(H, b), x2_done)
                if is_row(t, 0):
                    b = t
                    q3 = ps_qk[:, 0:2 * D].rearrange("p (h e) -> p h e", e=HD)
                    sp3 = sin_part[:, :].rearrange("p (h e) -> p h e", e=HD)
                    half = HD // 2
                    dve.wait_ge(qk_ps, b + 1)
                    if later(t, 0):
                        dve.wait_ge(qk_done, b)
                    dve.tensor_tensor(cos_part[:, :].rearrange("p (h e) -> p h e", e=HD), q3,
                                      cos_sb[:, :].unsqueeze(1).to_broadcast([T, 2 * HEADS, HD]), ALU.mult)\
                       .then_inc(rope_parts, 1)
                    dve.tensor_tensor(sp3[:, :, 0:half], q3[:, :, half:HD],
                                      sin_sb[:, 0:half].unsqueeze(1).to_broadcast([T, 2 * HEADS, half]),
                                      ALU.mult).then_inc(rope_parts, 1)
                    dve.tensor_tensor(sp3[:, :, half:HD], q3[:, :, 0:half],
                                      sin_sb[:, half:HD].unsqueeze(1).to_broadcast([T, 2 * HEADS, half]),
                                      ALU.mult).then_inc(rope_parts, 1)
                    dve.wait_ge(rope_parts, 3 * b + 3)
                    if later(t, 0):
                        dve.wait_ge(qkT_ps, b)
                    dve.tensor_tensor(qk[:, :], cos_part[:, :], sin_part[:, :], ALU.add).then_inc(qk_done, 1)
                if is_row(t, -LEAD_EMB):
                    b = t + LEAD_EMB
                    wait_apart(dve, emb_done, b + 1)
                    if later(t, -LEAD_EMB):
                        dve.wait_ge(norm0_done, b)
                    layer_stats(0, b, row(H, b))
                if is_row(t, LAG_PV):
                    b = t - LAG_PV
                    pv3 = ps_pv[:, 0:HEADS * VW].rearrange("p (h e) -> p h e", e=VW)
                    dve.wait_ge(pv_ps, b + 1)
                    dve.reciprocal(rsum[:, :].unsqueeze(2), pv3[:, :, HD:VW]).then_inc(rsum_done, 1)
                    dve.wait_ge(rsum_done, b + 1)
                    if later(t, LAG_PV):
                        dve.wait_ge(oT_ps, b)
                    dve.tensor_tensor(o[:, :].rearrange("p (h e) -> p h e", e=HD), pv3[:, :, 0:HD],
                                      rsum[:, :].unsqueeze(2).to_broadcast([T, HEADS, HD]), ALU.mult)\
                       .then_inc(o_done, 1)

            def mix_weights(t):
                if t == FIRST:
                    dve.wait_ge(ffn_in, 8 * 16)
                    dve.tensor_scalar(mix[:, 0:D], m_in_sb[:, :], alphas[:, 0:1], alphas[:, 1:2],
                                      ALU.mult, ALU.mult).then_inc(mix_done, 1)
                    dve.tensor_tensor(mix[:, D:D + 1], alphas[:, 0:1], alphas[:, 1:2], ALU.mult)\
                       .then_inc(mix_done, 1)
                for n in COEF_STEPS.get(t, ()):
                    dve.wait_ge(coef_ps, n + 1)
                    src = ps_c[n % 2]
                    if n < 4:
                        w = slice(n * HID // 2, (n + 1) * HID // 2)
                        dve.tensor_tensor(w0[:, w], fc_raw[:, w], src[0:KH, 0:HID // 2], ALU.mult)\
                           .then_inc(coef_used, 1)
                    elif n < 4 + HC:
                        m = n - 4
                        w = slice(m * D, (m + 1) * D)
                        dve.tensor_tensor(w1[:, w], proj_raw[:, w], src[:, 0:D], ALU.mult)
                        dve.tensor_tensor(b0[:, m:m + 1], bfc_sb[:, m:m + 1], src[:, D:D + 1], ALU.mult)\
                           .then_inc(coef_used, 1)
                    else:
                        dve.tensor_tensor(b1[:, :], bproj_sb[:, :], src[:, 0:D], ALU.mult)\
                           .then_inc(coef_used, 1)

            pipeline(dve, step, mix_weights)

            with dve.Fori(0, NG) as g:
                dve.wait_ge(h_used, g * HC + HC)
                dve.wait_ge(res_done, g + 1)
                for r in range(GROUP):
                    x = H[:, bass.ds(g * (GROUP * D) + r * D, D)]
                    dve.tensor_tensor(x, x, ps_y[r][:, 0:D], ALU.add).then_inc(y_done, 1)

        @block.tensor
        def _(pe):
            pe.wait_ge(attn_in, 3 * 16)
            for n in range(6):
                c, j = n % 2, n // 2
                pe.matmul(ps_w[n][0:KH, 0:D], projA[:, j * D + c * KH:j * D + (c + 1) * KH],
                          projB[:, j * D:(j + 1) * D], start=True, stop=True).then_inc(wqkv_ps, 1)
            pe.wait_ge(consts_done, 3)
            pe.wait_ge(wqkv_done, 6)

            def step(t):
                if is_row(t, LAG_S):
                    b = t - LAG_S
                    pe.wait_ge(qk_done, b + 1)
                    for c in range(4):
                        mm = pe.transpose(ps_qk[0:KH, c * T:(c + 1) * T], qk[:, c * KH:(c + 1) * KH], ident[:, :])
                    mm.then_inc(qkT_ps, 1)
                if is_row(t, 0):
                    b = t
                    pe.wait_ge(x1_done, b + 1)
                    if later(t, 0):
                        pe.wait_ge(v_done, b)
                    for c in range(2):
                        mm = pe.transpose(ps_v[0:KH, c * T:(c + 1) * T], x1[:, c * KH:(c + 1) * KH], ident[:, :])
                    mm.then_inc(x1T_ps, 1)
                if is_row(t, LAG_OW):
                    b = t - LAG_OW
                    pe.wait_ge(oT_done, b + 1)
                    if later(t, LAG_OW):
                        pe.wait_ge(x2T_done, b)
                    for c in range(2):
                        mm = pe.matmul(ps_ow[:, 0:D], oT[:, c * T:(c + 1) * T], wo_sb[:, c * D:(c + 1) * D],
                                       start=(c == 0), stop=(c == 1))
                    mm.then_inc(ow_ps, 1)
                if is_row(t, LAG_S):
                    b = t - LAG_S
                    pe.wait_ge(qkT_done, b + 1)
                    if later(t, LAG_S):
                        pe.wait_ge(pT_done, b)
                    for c in range(2):
                        for j in range(HPB):
                            pe.matmul(s_bank[j][:, c * T:(c + 1) * T], ident_b[:, :], causal[:, :],
                                      start=True, stop=False)
                        for j in range(HPB):
                            part = slice(j * HD, (j + 1) * HD)
                            mm = pe.matmul(s_bank[j][:, c * T:(c + 1) * T], qkT[part, c * T:(c + 1) * T],
                                           qkT[part, (2 + c) * T:(3 + c) * T], start=False,
                                           stop=True)
                    mm.then_inc(s_ps, 1)
                if is_row(t, 0):
                    b = t
                    pe.wait_ge(x1T_done, b + 1)
                    if later(t, 0):
                        pe.wait_ge(qkT_done, b)
                    for c in range(2):
                        mm = pe.matmul(ps_qk[:, 0:2 * D], x1T[:, c * T:(c + 1) * T],
                                       wqkv[:, c * 3 * D:c * 3 * D + 2 * D], start=(c == 0), stop=(c == 1))
                    mm.then_inc(qk_ps, 1)
                    for c in range(2):
                        mm = pe.matmul(ps_v[:, 0:D], x1T[:, c * T:(c + 1) * T],
                                       wqkv[:, c * 3 * D + 2 * D:(c + 1) * 3 * D], start=(c == 0), stop=(c == 1))
                    mm.then_inc(v_ps, 1)
                if is_row(t, LAG_PV):
                    b = t - LAG_PV
                    pe.wait_ge(pT_done, b + 1)
                    pe.wait_ge(v_done, b + 1)
                    if later(t, LAG_PV):
                        pe.wait_ge(oT_done, b)
                    for h in range(HEADS):
                        s = 2 * (h % HPB) + h // HPB
                        mm = pe.matmul(ps_pv[:, h * VW:(h + 1) * VW], pT[:, s * T:(s + 1) * T],
                                       vaug[:, bass.ds(b * (HEADS * VW) + h * VW, VW)], start=True, stop=True,
                                       skip_group_check=True)
                    mm.then_inc(pv_ps, 1)
                if is_row(t, LAG_OW):
                    b = t - LAG_OW
                    pe.wait_ge(x2_done, b + 1)
                    for c in range(2):
                        mm = pe.transpose(ps_ow[0:KH, c * T:(c + 1) * T], x2[:, c * KH:(c + 1) * KH], ident[:, :])
                    mm.then_inc(x2T_ps, 1)
                if is_row(t, LAG_S):
                    b = t - LAG_S
                    pe.wait_ge(p_done, b + 1)
                    for h in range(HEADS):
                        mm = pe.transpose(s_bank[h // 2][:, (h % 2) * T:(h % 2 + 1) * T],
                                          p[:, h * T:(h + 1) * T], ident[:, :])
                    mm.then_inc(pT_ps, 1)
                if is_row(t, LAG_PV):
                    b = t - LAG_PV
                    pe.wait_ge(o_done, b + 1)
                    for c in range(2):
                        mm = pe.transpose(ps_pv[0:KH, c * T:(c + 1) * T], o[:, c * KH:(c + 1) * KH], ident[:, :])
                    mm.then_inc(oT_ps, 1)

            def coefficients(t):
                for n in COEF_STEPS.get(t, ()):
                    pe.wait_ge(mix_done, 2)
                    if n >= 2:
                        pe.wait_ge(coef_used, n - 1)
                    dst = ps_c[n % 2]
                    if n < 4:
                        c, k, w = n // 2, n % 2, HID // 2
                        mm = pe.matmul(dst[0:KH, 0:w], mix[:, c * KH:(c + 1) * KH],
                                       m_out_sb[:, k * w:(k + 1) * w], start=True, stop=True)
                    elif n < 4 + HC:
                        m = n - 4
                        mm = pe.matmul(dst[:, 0:D + 1], m_out_sb[:, m * 128:(m + 1) * 128], mix[:, :],
                                       start=True, stop=True)
                    else:
                        mm = pe.matmul(dst[:, 0:D], ones9[:, :], mix[:, 0:D], start=True, stop=True)
                    mm.then_inc(coef_ps, 1)
                if t == LAG_OW - 1:
                    pe.wait_ge(coef_used, 4 + HC + 1)

            pipeline(pe, step, coefficients)

            pe.wait_ge(x2T_done, B)

            def hidden(g, m, n):
                if not isinstance(n, int) or n >= 3:
                    pe.wait_ge(h_done, n - 2)
                for c in range(2):
                    mm = pe.matmul(ps_h[m % 3][:, :], w0[:, c * HID + m * 128:c * HID + (m + 1) * 128],
                                   x2T[:, bass.ds(g * GT + c * (B * T), GT)], start=(c == 0), stop=(c == 1))
                mm.then_inc(h_ps, 1)

            def result(g, m):
                pe.wait_ge(h_done, g * HC + m + 1)
                if m == 0 and later(g, 0):
                    pe.wait_ge(y_done, g * GROUP)
                for r in range(GROUP):
                    mm = pe.matmul(ps_y[r][:, 0:D], hT[:, m * GT + r * T:m * GT + (r + 1) * T],
                                   w1[:, m * D:(m + 1) * D], start=(m == 0), stop=(m == HC - 1))
                mm.then_inc(h_used, 1)

            for m in range(HC):
                hidden(0, m, m)
            def overlapped(g):
                for m in range(HC):
                    hidden(g + 1, m, (g + 1) * HC + m)
                    result(g, m)

            overlapped(0)
            with pe.Fori(1, NG - 1) as g:
                overlapped(g)
            for m in range(HC):
                result(NG - 1, m)


def kernel(**inputs):
    import numpy as np
    import concourse.bacc as bacc
    from concourse.bass_utils import run_bass_kernel_spmd

    a = {k: np.asarray(v) for k, v in inputs.items()}
    t = lambda k: a[k].T
    f = np.float32
    inv = f(1.0) / np.power(f(10000.0), np.arange(0, HD, 2, dtype=f) / f(HD))
    angle = np.outer(np.arange(T, dtype=f), inv).astype(f)
    cos, sin = np.cos(angle).astype(f), np.sin(angle).astype(f)
    arrays = {
        "ids": t("x"),
        "seg": t("mask_BS_i1_0"),
        "tok_table": a["L0_tok_tok_table"],
        "seg_table": a["L0_tok_seg_table"].reshape(-1),
        "pos_table": a["L0_tok_pos_table"][:T],
        "gamma": a["L0_tok_gamma"],
        "beta": a["L0_tok_beta"],
        "qkvA": np.concatenate([t("L0_attn_qA"), t("L0_attn_kA"), t("L0_attn_vA")], axis=1),
        "qkvB": np.concatenate([a["L0_attn_qB"], a["L0_attn_kB"], a["L0_attn_vB"]], axis=1),
        "o_w": a["L0_attn_o_w"],
        "w_fc": t("L0_ffn_w_fc"),
        "b_fc": a["L0_ffn_b_fc"].reshape(HC, 128).T,
        "w_proj": t("L0_ffn_w_proj"),
        "b_proj": a["L0_ffn_b_proj"],
        "alpha_e": np.repeat(a["L0_ffn_alpha_e"], len(RATIOS))[:, None],
        "alpha_r": np.tile(a["L0_ffn_alpha_r"], len(EMBEDS))[:, None],
        "m_in": np.array([[d < e for d in range(D)] for e in EMBEDS for _ in RATIOS], dtype=f),
        "m_out": np.array([[h < r * e for h in range(HID)] for e in EMBEDS for r in RATIOS], dtype=f),
        "rope_cos": np.concatenate([cos, cos], axis=1),
        "rope_sin": np.concatenate([-sin, sin], axis=1),
    }
    arrays = {k: np.ascontiguousarray(v) for k, v in arrays.items()}
    nc = bacc.Bacc("TRN2", target_bir_lowering=False, num_devices=1)
    args = [nc.dram_tensor(f"in_{k}", v.shape, mybir.dt.from_np(v.dtype), kind="ExternalInput").ap()
            for k, v in arrays.items()]
    out = nc.dram_tensor("out_0", (B, T, D), mybir.dt.float32, kind="ExternalOutput").ap()
    lm_layer(nc, *args, out)
    r = run_bass_kernel_spmd(nc, [{f"in_{k}": v for k, v in arrays.items()}], core_ids=[0])
    return r.results[0]["out_0"]
```

```python
import concourse.bass as bass
from concourse import mybir
from contextlib import ExitStack

B, T, D = 16, 128, 192
HEADS, HD = 6, 32
RANK = 48
HID = 768
KH = D // 2
KC = 2 * D // 128
PARTS = [(k, 128, "hi") for k in range(KC)] + [(0, 128, "lo"), (1, D - 128, "lo")]
HPB = HEADS // 2
PB = 512
VW = HD + 1
GROUP = 4
NG = B // GROUP
GT = GROUP * T
HC = HID // 128
EPS = 1e-5
MASKED = -1e30
SCALE = float(HD) ** -0.5
EMBEDS, RATIOS = (96, 144, 192), (2, 3, 4)
NC9 = len(EMBEDS) * len(RATIOS)

LAG_S, LAG_PV, LAG_OW, LAG_X2 = 1, 2, 3, 4
LEAD_EMB, LEAD_ST0, LEAD_LN0, LEAD_LN1 = 4, 3, 2, 1
FIRST, LAST = -LEAD_EMB, B - 1 + LAG_X2
N0 = 2 * KC
NCOEF = N0 + HC + 1
AHEAD = 4
EARLY = 0
COEF_STEPS = {-2: range(0, 6), -1: range(6, 8), 0: range(8, 10), 1: range(10, NCOEF)}
SPLIT_STEPS = {B - LEAD_EMB: range(0, 4), B - LEAD_EMB + 1: range(4, N0 + 2),
               B - LEAD_EMB + 2: range(N0 + 2, N0 + 4), B - LEAD_EMB + 3: range(N0 + 4, NCOEF)}
STEADY = (LAG_X2 + 1, B - LEAD_EMB)
HID_STEP = B - 1 + LAG_S


def lm_layer(nc, ids_seg, tok_table, rows_in, pos_rope, qkv_low_rank, o_w, w_fc, b_fc, w_proj, mixing, out):
    fp32, bf16, f32r = mybir.dt.float32, mybir.dt.bfloat16, mybir.dt.float32r
    ALU, ACT, AX = mybir.AluOpType, mybir.ActivationFunctionType, mybir.AxisListType
    ctx = ExitStack()
    with ctx:
        def sb(name, shape, dt=fp32):
            return ctx.enter_context(nc.sbuf_tensor(name, shape, dt))

        def sem(name):
            return ctx.enter_context(nc.semaphore(name))

        ids_seg_sb = sb("ids_seg_sb", [T, 2 * B], mybir.dt.int32)
        ids_sb, seg_i = ids_seg_sb[:, 0:B], ids_seg_sb[:, B:2 * B]
        seg_f = sb("seg_f", [T, B])
        rows_sb = sb("rows_sb", [T, 5 * D])
        seg_rows, gamma_sb, beta_sb = rows_sb[:, 0:2 * D], rows_sb[:, 2 * D:3 * D], rows_sb[:, 3 * D:4 * D]
        bproj_sb = rows_sb[:, 4 * D:5 * D]
        seg_diff = sb("seg_diff", [T, D])
        pos_rope_sb = sb("pos_rope_sb", [T, D + 2 * HD])
        pos_sb, cos_sb = pos_rope_sb[:, 0:D], pos_rope_sb[:, D:D + HD]
        sin_sb = pos_rope_sb[:, D + HD:D + 2 * HD]
        proj_sb = sb("proj_sb", [RANK, 3 * 2 * D + 3 * D])
        projA, projB = proj_sb[:, 0:3 * 2 * D], proj_sb[:, 3 * 2 * D:3 * 3 * D]
        wqkv = {"hi": sb("wqkv_hi", [128, KC * 3 * D], f32r), "lo": sb("wqkv_lo", [128, 2 * 3 * D], f32r)}
        wo_sb = sb("wo_sb", [KH, 2 * D])
        w0 = sb("w0", [128, KC * HID])
        w0_part = {"hi": sb("w0_hi", [128, KC * HID], f32r), "lo": sb("w0_lo", [128, 2 * HID], f32r)}
        w1 = sb("w1", [128, HC * D])
        w1_parts = sb("w1_parts", [128, HC * 2 * D], f32r)
        bfc_sb = sb("bfc_sb", [128, HC])
        b0 = sb("b0", [128, HC])
        b1 = sb("b1", [T, D])
        mixing_sb = sb("mixing_sb", [NC9, 2 * D + HID + 2])
        m_in_sb, m_out_sb = mixing_sb[:, 0:2 * D], mixing_sb[:, 2 * D:2 * D + HID]
        alphas = mixing_sb[:, 2 * D + HID:]
        mix = sb("mix", [NC9, 2 * D + 1])
        ones9 = sb("ones9", [NC9, T])
        coef0 = sb("coef0", [128, KC * HID])
        coef1 = sb("coef1", [128, HC * (D + 1)])
        coef_b = sb("coef_b", [T, D])
        ident = sb("ident", [128, 128])
        ident_b = sb("ident_b", [128, 128], bf16)
        causal = sb("causal", [128, T], bf16)
        half_neg = sb("half_neg", [T, 1])
        eps_sb = sb("eps_sb", [T, 1])

        H = sb("H", [T, B * D])
        seg_add = sb("seg_add", [T, D])
        emb_sum = sb("emb_sum", [T, D])
        bn = [sb(f"bn{k}", [T, 6]) for k in range(3)]
        mv = [sb(f"mv{k}", [T, 2]) for k in range(3)]
        ve = [sb(f"ve{k}", [T, 1]) for k in range(3)]
        rstd = [sb(f"rstd{k}", [T, 1]) for k in range(3)]
        x1 = sb("x1", [T, D])
        x1_parts = sb("x1_parts", [T, 2 * D])
        x1T = sb("x1T", [128, KC * T], f32r)
        cos_part = sb("cos_part", [T, 2 * D])
        sin_part = sb("sin_part", [T, 2 * D])
        qk = sb("qk", [T, 2 * D])
        qkT = sb("qkT", [KH, 4 * T])
        vaug = sb("vaug", [T, B * HEADS * VW])
        smax = sb("smax", [T, HEADS])
        nmax = sb("nmax", [T, HEADS])
        p = sb("p", [T, HEADS * T])
        pT = sb("pT", [T, HEADS * T])
        rsum = sb("rsum", [T, HEADS])
        o = sb("o", [T, D])
        oT = sb("oT", [KH, 2 * T])
        x2 = sb("x2", [T, D])
        x2_parts = sb("x2_parts", [T, 2 * D])
        x2T = sb("x2T", [128, KC * B * T], f32r)
        h_act = [sb(f"h_act{k}", [128, GT]) for k in range(2)]
        hT = {"hi": sb("hT_hi", [128, HC * GT], f32r), "lo": sb("hT_lo", [128, HC * GT], f32r)}

        def pb(name, banks=1):
            return ctx.enter_context(nc.psum_tensor(name, [128, banks * PB], fp32))

        ps_qk, ps_v, ps_pv, ps_ow, ps_x = (pb(f"ps_{n}")[:, :] for n in ("qk", "v", "pv", "ow", "x"))
        ps_s = pb("ps_s", HPB)
        s_bank = [ps_s[:, j * PB:(j + 1) * PB] for j in range(HPB)]
        s_all = ps_s[:, :].rearrange("p (j n) -> p j n", j=HPB)[:, :, 0:2 * T]
        ps_w = [ps_qk, ps_v, *s_bank, ps_pv]
        ps_c = [ps_ow, ps_x]
        ps_h = [ps_x, *s_bank[:2]]
        ps_y = [ps_qk, ps_v, ps_pv, ps_ow]

        ids_in = sem("ids_in")
        emb_in = sem("emb_in")
        attn_in = sem("attn_in")
        mixing_in = sem("mixing_in")
        ffn_in = sem("ffn_in")
        tok_in = [sem(f"tok_in{b}") for b in range(B)]
        tok_rows = sem("tok_rows")
        pool_c = sem("pool_c")
        consts_done = sem("consts_done")
        seg_done = sem("seg_done")
        wqkv_ps = sem("wqkv_ps")
        wqkv_hi = sem("wqkv_hi")
        wqkv_lo = sem("wqkv_lo")
        w_hi = sem("w_hi")
        w_lo = sem("w_lo")
        mix_done = sem("mix_done")
        coef_ps = sem("coef_ps")
        coef_done = sem("coef_done")
        mixed = sem("mixed")
        emb_done = sem("emb_done")
        stats = [sem(f"stats{k}") for k in range(3)]
        rstd_done = [sem(f"rstd_done{k}") for k in range(3)]
        ve_done = [sem(f"ve_done{k}") for k in range(3)]
        bn_done = [sem(f"bn_done{k}") for k in range(3)]
        seg_added = sem("seg_added")
        emb_summed = sem("emb_summed")
        scaled = sem("scaled")
        h1_done = sem("h1_done")
        rope_parts = sem("rope_parts")
        smax_done = sem("smax_done")
        rsum_done = sem("rsum_done")
        norm0_done = sem("norm0_done")
        h0_done = sem("h0_done")
        x1_norm = sem("x1_norm")
        x1_hi = sem("x1_hi")
        x1_done = sem("x1_done")
        x1T_ps = sem("x1T_ps")
        x1T_done = sem("x1T_done")
        qk_ps = sem("qk_ps")
        v_ps = sem("v_ps")
        v_done = sem("v_done")
        qk_done = sem("qk_done")
        qkT_ps = sem("qkT_ps")
        qkT_done = sem("qkT_done")
        s_ps = sem("s_ps")
        max_done = sem("max_done")
        p_done = sem("p_done")
        pT_ps = sem("pT_ps")
        pT_done = sem("pT_done")
        pv_ps = sem("pv_ps")
        o_done = sem("o_done")
        oT_ps = sem("oT_ps")
        oT_done = sem("oT_done")
        ow_ps = sem("ow_ps")
        x2_norm = sem("x2_norm")
        x2_hi = sem("x2_hi")
        x2_done = sem("x2_done")
        x2T_ps = sem("x2T_ps")
        x2T_done = sem("x2T_done")
        res_done = sem("res_done")
        h_ps = sem("h_ps")
        h_done = sem("h_done")
        h_hi = sem("h_hi")
        h_split = sem("h_split")
        h_used = sem("h_used")
        row_ps = sem("row_ps")
        half_added = sem("half_added")
        y_done = sem("y_done")
        stored = sem("stored")

        block = ctx.enter_context(nc.Block())

        def row(t, b):
            return t[:, bass.ts(b, D)]

        def pipeline(eng, step, after=None):
            for t in range(FIRST, STEADY[0]):
                step(t)
                if after:
                    after(t)
            with eng.Fori(STEADY[0], STEADY[1]) as t:
                step(t)
            for t in range(STEADY[1], LAST + 1):
                step(t)
                if after:
                    after(t)

        def wait_apart(eng, sem, count):
            if not isinstance(count, int):
                eng.wait_ge(sem, 1)
            eng.wait_ge(sem, count)

        def is_row(t, d):
            return not isinstance(t, int) or 0 <= t - d < B

        def later(t, d=0):
            return not isinstance(t, int) or t - d >= 1

        def early(t):
            return isinstance(t, int) and t < EARLY

        def embed(eng, b):
            eng.tensor_tensor(seg_add[:, :], seg_diff[:, :],
                              seg_f[:, bass.ds(b, 1)].to_broadcast([T, D]), ALU.mult).then_inc(seg_added, 1)
            wait_apart(eng, seg_added, b + 1)
            eng.tensor_tensor(emb_sum[:, :], seg_add[:, :], pos_sb, ALU.add).then_inc(emb_summed, 1)
            wait_apart(eng, emb_summed, b + 1)
            eng.wait_ge(tok_rows, b + 1)
            eng.tensor_tensor(row(H, b), row(H, b), emb_sum[:, :], ALU.add).then_inc(emb_done, 1)

        def scale_shift(eng, b):
            wait_apart(eng, norm0_done, b + 1)
            eng.tensor_tensor(row(H, b), row(H, b), gamma_sb, ALU.mult).then_inc(scaled, 1)
            wait_apart(eng, scaled, b + 1)
            eng.tensor_tensor(row(H, b), row(H, b), beta_sb, ALU.add).then_inc(h0_done, 1)

        def first_chunks(t):
            return range(HC)[2 * (t - HID_STEP):2 * (t - HID_STEP) + 2] if t >= HID_STEP else ()

        def chunk0(k, half):
            return slice(k * HID + half * HID // 2, k * HID + (half + 1) * HID // 2)

        @block.sync
        def _(sp):
            sp.dma_start(ids_seg_sb[:, :], ids_seg).then_inc(ids_in, 16)
            sp.dma_start(rows_sb[:, :], rows_in.partition_broadcast(T)).then_inc(emb_in, 16)
            sp.dma_start(mixing_sb[:, :], mixing).then_inc(mixing_in, 16)
            for b in range(B):
                sp.wait_ge(tok_in[b], 16)
                sp.sem_inc(tok_rows, 1)
                if b == AHEAD - 1:
                    sp.dma_start(w0[:, :].rearrange("p (k n) -> p k n", k=KC),
                                 w_fc.rearrange("(k p) n -> p k n", p=128)).then_inc(ffn_in, 16)
                    sp.dma_start(w1[:, :].rearrange("p (c n) -> p c n", c=HC),
                                 w_proj.rearrange("(c p) n -> p c n", p=128)).then_inc(ffn_in, 16)
                    sp.dma_start(bfc_sb[:, :], b_fc).then_inc(ffn_in, 16)
            with sp.Fori(0, NG - 1) as g:
                sp.wait_ge(y_done, g * GROUP + GROUP)
                sp.dma_start(out[bass.ts(g, GROUP), :, :].rearrange("b t d -> t b d"),
                             H[:, bass.ts(g, GROUP * D)].rearrange("t (b d) -> t b d", d=D))\
                  .then_inc(stored, 16)
            for b in range(B - GROUP, B):
                sp.wait_ge(y_done, b + 1)
                sp.dma_start(out[b, :, :], row(H, b)).then_inc(stored, 16)
            sp.wait_ge(stored, 16 * (NG - 1 + GROUP))

        @block.gpsimd
        def _(pool):
            pool.wait_ge(ids_in, 16)

            def gather(b):
                pool.indirect_dma_start(out=row(H, b), out_offset=None, in_=tok_table,
                                        in_offset=bass.IndirectOffsetOnAxis(ap=ids_sb[:, b:b + 1], axis=0))\
                    .then_inc(tok_in[b], 16)

            for b in range(AHEAD):
                gather(b)
            pool.memset(ident[:, :], 0.0).then_inc(pool_c, 1)
            pool.memset(ident_b[:, :], 0.0).then_inc(pool_c, 1)
            pool.memset(causal[:, :], 0.0).then_inc(pool_c, 1)
            pool.memset(vaug[:, :].rearrange("p (n e) -> p n e", e=VW)[:, :, HD:VW], 1.0).then_inc(pool_c, 1)
            pool.memset(half_neg[:, :], -0.5).then_inc(pool_c, 1)
            pool.memset(eps_sb[:, :], EPS).then_inc(pool_c, 1)
            pool.memset(ones9[:, :], 1.0).then_inc(pool_c, 1)
            pool.wait_ge(pool_c, 7)
            for m in (ident, ident_b):
                pool.affine_select(out=m[:, :], in_=m[:, :], compare_op=ALU.not_equal, fill=1.0, base=0,
                                   pattern=[[-1, 128]], channel_multiplier=1).then_inc(consts_done, 1)
            pool.affine_select(out=causal[:, :], in_=causal[:, :], compare_op=ALU.is_ge, fill=MASKED, base=0,
                               pattern=[[-1, T]], channel_multiplier=1).then_inc(consts_done, 1)
            def inv_std(k, b):
                wait_apart(pool, stats[k], b + 1)
                pool.tensor_tensor(ve[k][:, :], mv[k][:, 1:2], eps_sb[:, :], ALU.add).then_inc(ve_done[k], 1)
                pool.wait_ge(ve_done[k], b + 1)
                pool.tensor_tensor(rstd[k][:, :], ve[k][:, :], half_neg[:, :], ALU.pow)\
                    .then_inc(rstd_done[k], 1)

            def step(t):
                if is_row(t, -LEAD_LN0) and not early(t):
                    scale_shift(pool, t + LEAD_LN0)
                if is_row(t, -LEAD_ST0):
                    inv_std(0, t + LEAD_ST0)
                if is_row(t, -LEAD_EMB) and not early(t):
                    if isinstance(t, int) and t == EARLY:
                        pool.wait_ge(emb_done, t + LEAD_EMB)
                    embed(pool, t + LEAD_EMB)
                if is_row(t, LAG_OW):
                    inv_std(2, t - LAG_OW)
                if is_row(t, -LEAD_LN0):
                    inv_std(1, t + LEAD_LN0)

            def between(t):
                begin = AHEAD + (t - FIRST if t < 0 else -FIRST + 2 * t)
                for b in range(begin, min(begin + (1 if t < 0 else 2), B)):
                    gather(b)
                for n in SPLIT_STEPS.get(t, ()):
                    if n < N0 + HC:
                        pool.wait_ge(w_hi, n + 1)
                    if n < 4:
                        w, rows = chunk0(n // 2, n % 2), 128 if n < 2 else D - 128
                        pool.tensor_tensor(w0_part["lo"][0:rows, w], w0[0:rows, w],
                                           w0_part["hi"][0:rows, w].bitcast(fp32), ALU.subtract).then_inc(w_lo, 1)
                    elif N0 <= n < N0 + HC:
                        m = n - N0
                        pool.tensor_tensor(w1_parts[:, (2 * m + 1) * D:(2 * m + 2) * D], w1[:, m * D:(m + 1) * D],
                                           w1_parts[:, 2 * m * D:(2 * m + 1) * D].bitcast(fp32), ALU.subtract)\
                            .then_inc(w_lo, 1)

            pipeline(pool, step, between)

            pool.wait_ge(mixed, NCOEF)
            with pool.Fori(0, NG) as g:
                wait_apart(pool, x2_done, g * GROUP + GROUP)
                rows = H[:, bass.ts(g, GROUP * D)].rearrange("t (b d) -> t b d", d=D)
                pool.tensor_tensor(rows, rows, b1[:, :].unsqueeze(1).to_broadcast([T, GROUP, D]), ALU.add)\
                    .then_inc(res_done, 1)

        @block.scalar
        def _(act):
            act.dma_start(pos_rope_sb[:, :], pos_rope).then_inc(emb_in, 16)
            act.dma_start(proj_sb[:, :], qkv_low_rank).then_inc(attn_in, 16)
            act.dma_start(wo_sb[:, :].rearrange("p (c n) -> p c n", c=2),
                          o_w.rearrange("(c p) n -> p c n", p=KH)).then_inc(attn_in, 16)
            for n in range(2 * KC):
                w = slice(n // 2 * 3 * D + n % 2 * 2 * D, n // 2 * 3 * D + (2 + n % 2) * D)
                act.wait_ge(wqkv_ps, n + 1)
                act.copy(wqkv["hi"][:, w], ps_w[n][:, 0:(2 - n % 2) * D]).then_inc(wqkv_hi, 1)

            def coefficients_out(n):
                act.wait_ge(coef_ps, n + 1)
                if n < N0:
                    dst, w = coef0[:, chunk0(n // 2, n % 2)], HID // 2
                elif n < N0 + HC:
                    dst, w = coef1[:, (n - N0) * (D + 1):(n - N0 + 1) * (D + 1)], D + 1
                else:
                    dst, w = coef_b[:, :], D
                act.copy(dst, ps_c[n % 2][:, 0:w]).then_inc(coef_done, 1)

            def high_part(dst, x):
                return act.copy(dst[:, 0:D].bitcast(f32r), x[:, :])

            def step(t):
                if is_row(t, LAG_X2):
                    b = t - LAG_X2
                    act.wait_ge(x2_norm, b + 1)
                    if later(t, LAG_X2):
                        act.wait_ge(x2T_ps, b)
                    high_part(x2_parts, x2).then_inc(x2_hi, 1)
                if is_row(t, -LEAD_LN1):
                    b = t + LEAD_LN1
                    act.wait_ge(x1_norm, b + 1)
                    if later(t, -LEAD_LN1):
                        act.wait_ge(x1T_ps, b)
                    high_part(x1_parts, x1).then_inc(x1_hi, 1)
                if is_row(t, 0):
                    b = t
                    act.wait_ge(v_ps, b + 1)
                    act.copy(vaug[:, bass.ts(b, HEADS * VW)].rearrange("p (h e) -> p h e", e=VW)[:, :, 0:HD],
                             ps_v[:, 0:D].rearrange("p (h e) -> p h e", e=HD)).then_inc(v_done, 1)
                if is_row(t, LAG_S):
                    b = t - LAG_S
                    act.wait_ge(max_done, b + 1)
                    if later(t, LAG_S):
                        act.wait_ge(pT_ps, b)
                    for h in range(HEADS):
                        e = act.activation(p[:, h * T:(h + 1) * T],
                                           s_bank[h // 2][:, (h % 2) * T:(h % 2 + 1) * T],
                                           ACT.Exp, bias=nmax[:, h:h + 1], scale=SCALE)
                    e.then_inc(p_done, 1)
                if is_row(t, -LEAD_LN1):
                    b = t + LEAD_LN1
                    act.wait_ge(x1T_ps, b + 1)
                    if later(t, -LEAD_LN1):
                        act.wait_ge(qk_ps, b)
                    act.copy(x1T[:, :], ps_v[:, 0:KC * T]).then_inc(x1T_done, 1)
                if is_row(t, 0):
                    b = t
                    act.wait_ge(qkT_ps, b + 1)
                    if later(t):
                        act.wait_ge(s_ps, b)
                    act.copy(qkT[:, :], ps_qk[0:KH, 0:4 * T]).then_inc(qkT_done, 1)
                if is_row(t, LAG_S):
                    b = t - LAG_S
                    act.wait_ge(pT_ps, b + 1)
                    if later(t, LAG_S):
                        act.wait_ge(pv_ps, b)
                    act.copy(pT[:, :].rearrange("p (j n) -> p j n", j=HPB), s_all).then_inc(pT_done, 1)
                if is_row(t, LAG_PV):
                    b = t - LAG_PV
                    act.wait_ge(oT_ps, b + 1)
                    if later(t, LAG_PV):
                        act.wait_ge(ow_ps, b)
                    act.copy(oT[:, :], ps_pv[0:KH, 0:2 * T]).then_inc(oT_done, 1)
                if is_row(t, LAG_X2):
                    b = t - LAG_X2
                    act.wait_ge(x2T_ps, b + 1)
                    act.copy(x2T[:, :].rearrange("p (k n) -> p k n", k=KC)[:, :, bass.ts(b, T)],
                             ps_ow[:, 0:KC * T].rearrange("p (k n) -> p k n", k=KC)).then_inc(x2T_done, 1)

            def gelu(g, m):
                act.wait_ge(h_ps, g * HC + m + 1)
                if m >= 2 or later(g, 0):
                    act.wait_ge(h_split, g * HC + m - 1)
                act.activation(h_act[m % 2][:, :], ps_h[m % 3][:, :], ACT.Gelu_apprx_tanh,
                               bias=b0[:, m:m + 1]).then_inc(h_done, 1)

            def between(t):
                for n in COEF_STEPS.get(t, ()):
                    coefficients_out(n)
                for n in SPLIT_STEPS.get(t, ()):
                    act.wait_ge(mixed, n + 1)
                    if n < N0:
                        w = chunk0(n // 2, n % 2)
                        act.copy(w0_part["hi"][:, w], w0[:, w]).then_inc(w_hi, 1)
                    elif n < N0 + HC:
                        m = n - N0
                        act.copy(w1_parts[:, 2 * m * D:(2 * m + 1) * D], w1[:, m * D:(m + 1) * D])\
                           .then_inc(w_hi, 1)
                for m in first_chunks(t):
                    gelu(0, m)

            pipeline(act, step, between)

            with act.Fori(1, NG) as g:
                for m in range(HC):
                    gelu(g, m)

        @block.vector
        def _(dve):
            dve.wait_ge(ids_in, 16)
            dve.wait_ge(emb_in, 2 * 16)
            dve.tensor_copy(seg_f[:, :], seg_i).then_inc(seg_done, 1)
            dve.tensor_tensor(pos_sb, pos_sb, seg_rows[:, 0:D], ALU.add).then_inc(seg_done, 1)
            dve.tensor_tensor(seg_diff[:, :], seg_rows[:, D:2 * D], seg_rows[:, 0:D], ALU.subtract)\
               .then_inc(seg_done, 1)
            dve.wait_ge(mixing_in, 16)
            dve.tensor_scalar(mix[:, 0:2 * D], m_in_sb, alphas[:, 0:1], alphas[:, 1:2],
                              ALU.mult, ALU.mult).then_inc(mix_done, 1)
            dve.tensor_tensor(mix[:, 2 * D:2 * D + 1], alphas[:, 0:1], alphas[:, 1:2], ALU.mult)\
               .then_inc(mix_done, 1)
            dve.wait_ge(seg_done, 3)

            def layer_stats(k, b, x):
                dve.bn_stats(bn[k][:, :], x).then_inc(bn_done[k], 1)
                wait_apart(dve, bn_done[k], b + 1)
                dve.bn_aggr(mv[k][:, :], bn[k][:, :]).then_inc(stats[k], 1)

            def normalize(k, b, dst, x, done):
                dve.wait_ge(rstd_done[k], b + 1)
                dve.tensor_scalar(dst, x, mv[k][:, 0:1], rstd[k][:, 0:1], ALU.subtract, ALU.mult)\
                   .then_inc(done, 1)

            def low_part(dst, x, hi, b):
                dve.wait_ge(hi, b + 1)
                return dve.tensor_tensor(dst[:, D:2 * D].bitcast(f32r), x[:, :], dst[:, 0:D], ALU.subtract)

            def step(t):
                if is_row(t, -LEAD_LN0):
                    b = t + LEAD_LN0
                    normalize(0, b, row(H, b), row(H, b), norm0_done)
                    if early(t):
                        scale_shift(dve, b)
                if is_row(t, LAG_X2):
                    b = t - LAG_X2
                    normalize(2, b, x2[:, :], row(H, b), x2_norm)
                if is_row(t, -LEAD_LN1):
                    b = t + LEAD_LN1
                    normalize(1, b, x1[:, :], row(H, b), x1_norm)
                if is_row(t, -LEAD_EMB) and early(t):
                    embed(dve, t + LEAD_EMB)
                if is_row(t, -LEAD_ST0):
                    b = t + LEAD_ST0
                    wait_apart(dve, emb_done, b + 1)
                    if later(t, -LEAD_ST0):
                        dve.wait_ge(norm0_done, b)
                    layer_stats(0, b, row(H, b))
                if is_row(t, LAG_X2):
                    b = t - LAG_X2
                    low_part(x2_parts, x2, x2_hi, b).then_inc(x2_done, 1)
                if is_row(t, -LEAD_LN1):
                    b = t + LEAD_LN1
                    low_part(x1_parts, x1, x1_hi, b).then_inc(x1_done, 1)
                if is_row(t, 0):
                    b = t
                    q3 = ps_qk[:, 0:2 * D].rearrange("p (h e) -> p h e", e=HD)
                    sp3 = sin_part[:, :].rearrange("p (h e) -> p h e", e=HD)
                    half = HD // 2
                    dve.wait_ge(qk_ps, b + 1)
                    if later(t, 0):
                        dve.wait_ge(qk_done, b)
                    dve.tensor_tensor(cos_part[:, :].rearrange("p (h e) -> p h e", e=HD), q3,
                                      cos_sb.unsqueeze(1).to_broadcast([T, 2 * HEADS, HD]), ALU.mult)\
                       .then_inc(rope_parts, 1)
                    dve.tensor_tensor(sp3[:, :, 0:half], q3[:, :, half:HD],
                                      sin_sb[:, 0:half].unsqueeze(1).to_broadcast([T, 2 * HEADS, half]),
                                      ALU.mult).then_inc(rope_parts, 1)
                    dve.tensor_tensor(sp3[:, :, half:HD], q3[:, :, 0:half],
                                      sin_sb[:, half:HD].unsqueeze(1).to_broadcast([T, 2 * HEADS, half]),
                                      ALU.mult).then_inc(rope_parts, 1)
                    dve.wait_ge(rope_parts, 3 * b + 3)
                    if later(t, 0):
                        dve.wait_ge(qkT_ps, b)
                    dve.tensor_tensor(qk[:, :], cos_part[:, :], sin_part[:, :], ALU.add).then_inc(qk_done, 1)
                if is_row(t, LAG_S):
                    b = t - LAG_S
                    dve.wait_ge(s_ps, b + 1)
                    dve.tensor_reduce(smax[:, :].rearrange("p (j c) -> p j c", c=2),
                                      s_all.rearrange("p j (c k) -> p j c k", k=T), AX.X, ALU.max)\
                       .then_inc(smax_done, 1)
                    dve.wait_ge(smax_done, b + 1)
                    if later(t, LAG_S):
                        dve.wait_ge(p_done, b)
                    dve.tensor_scalar(nmax[:, :], smax[:, :], -SCALE, None, ALU.mult).then_inc(max_done, 1)
                if is_row(t, LAG_PV):
                    b = t - LAG_PV
                    pv3 = ps_pv[:, 0:HEADS * VW].rearrange("p (h e) -> p h e", e=VW)
                    dve.wait_ge(pv_ps, b + 1)
                    dve.reciprocal(rsum[:, :].unsqueeze(2), pv3[:, :, HD:VW]).then_inc(rsum_done, 1)
                    dve.wait_ge(rsum_done, b + 1)
                    if later(t, LAG_PV):
                        dve.wait_ge(oT_ps, b)
                    dve.tensor_tensor(o[:, :].rearrange("p (h e) -> p h e", e=HD), pv3[:, :, 0:HD],
                                      rsum[:, :].unsqueeze(2).to_broadcast([T, HEADS, HD]), ALU.mult)\
                       .then_inc(o_done, 1)
                if is_row(t, LAG_OW):
                    b = t - LAG_OW
                    dve.wait_ge(ow_ps, b + 1)
                    dve.tensor_tensor(row(H, b), row(H, b), ps_ow[:, 0:D], ALU.add).then_inc(h1_done, 1)
                    wait_apart(dve, h1_done, b + 1)
                    if later(t, LAG_OW):
                        dve.wait_ge(x2_norm, b)
                    layer_stats(2, b, row(H, b))
                if is_row(t, -LEAD_LN0):
                    b = t + LEAD_LN0
                    wait_apart(dve, h0_done, b + 1)
                    if later(t, -LEAD_LN0):
                        dve.wait_ge(x1_norm, b)
                    layer_stats(1, b, row(H, b))

            def mix_weights(n):
                dve.wait_ge(ffn_in, 3 * 16)
                dve.wait_ge(coef_done, n + 1)
                if n < N0:
                    w = chunk0(n // 2, n % 2)
                    dve.tensor_tensor(w0[:, w], w0[:, w], coef0[:, w], ALU.mult).then_inc(mixed, 1)
                elif n < N0 + HC:
                    m = n - N0
                    w, c = slice(m * D, (m + 1) * D), m * (D + 1)
                    dve.tensor_tensor(b0[:, m:m + 1], bfc_sb[:, m:m + 1], coef1[:, c + D:c + D + 1], ALU.mult)
                    dve.tensor_tensor(w1[:, w], w1[:, w], coef1[:, c:c + D], ALU.mult).then_inc(mixed, 1)
                else:
                    dve.tensor_tensor(b1[:, :], bproj_sb, coef_b[:, :], ALU.mult).then_inc(mixed, 1)

            def split_hidden(g, m):
                w, x = slice(m * GT, (m + 1) * GT), h_act[m % 2][:, :]
                dve.wait_ge(h_done, g * HC + m + 1)
                if later(g, 0):
                    dve.wait_ge(h_used, (g - 1) * HC + m + 1)
                dve.tensor_copy(hT["hi"][:, w], x).then_inc(h_hi, 1)
                dve.wait_ge(h_hi, g * HC + m + 1)
                dve.tensor_tensor(hT["lo"][:, w], x, hT["hi"][:, w].bitcast(fp32), ALU.subtract)\
                   .then_inc(h_split, 1)

            def fold_low_parts():
                for n in range(4):
                    rows = slice(0, 128 if n < 2 else D - 128)
                    w = slice(n // 2 * 3 * D + n % 2 * 2 * D, n // 2 * 3 * D + (2 + n % 2) * D)
                    dve.wait_ge(wqkv_hi, n + 1)
                    dve.tensor_tensor(wqkv["lo"][rows, w], ps_w[n][rows, 0:(2 - n % 2) * D],
                                      wqkv["hi"][rows, w].bitcast(fp32), ALU.subtract).then_inc(wqkv_lo, 1)

            def between(t):
                if t == -3:
                    fold_low_parts()
                for n in SPLIT_STEPS.get(t, ()):
                    mix_weights(n)
                for m in first_chunks(t - 1):
                    split_hidden(0, m)

            pipeline(dve, step, between)

            def residual(g, r):
                x = row(H, g * GROUP + r)
                dve.tensor_tensor(x, x, ps_y[r][:, 0:D], ALU.add).then_inc(half_added, 1)
                dve.wait_ge(half_added, g * GROUP + r + 1)
                dve.tensor_tensor(x, x, ps_y[r][:, D:2 * D], ALU.add).then_inc(y_done, 1)

            with dve.Fori(0, NG - 1) as g:
                for m in range(HC - 1):
                    split_hidden(g + 1, m)
                dve.wait_ge(h_used, g * HC + HC)
                dve.wait_ge(res_done, g + 1)
                for r in range(GROUP):
                    residual(g, r)
                split_hidden(g + 1, HC - 1)
            dve.wait_ge(res_done, NG)
            for r in range(GROUP):
                dve.wait_ge(row_ps, r + 1)
                residual(NG - 1, r)

        @block.tensor
        def _(pe):
            pe.wait_ge(attn_in, 2 * 16)
            for n in range(2 * KC):
                k = n // 2
                for i, j in enumerate((0, 1) if n % 2 == 0 else (2,)):
                    mm = pe.matmul(ps_w[n][:, i * D:(i + 1) * D],
                                   projA[:, j * 2 * D + k * 128:j * 2 * D + (k + 1) * 128],
                                   projB[:, j * D:(j + 1) * D], start=True, stop=True)
                mm.then_inc(wqkv_ps, 1)
            pe.wait_ge(mix_done, 2)
            pe.wait_ge(consts_done, 3)

            def coefficients(n):
                if n >= 2:
                    pe.wait_ge(coef_done, n - 1)
                dst = ps_c[n % 2]
                if n < N0:
                    k, half = n // 2, n % 2
                    mm = pe.matmul(dst[:, 0:HID // 2], mix[:, k * 128:(k + 1) * 128],
                                   m_out_sb[:, half * HID // 2:(half + 1) * HID // 2], start=True, stop=True)
                elif n < N0 + HC:
                    m = n - N0
                    mm = pe.matmul(dst[:, 0:D + 1], m_out_sb[:, m * 128:(m + 1) * 128], mix[:, D:2 * D + 1],
                                   start=True, stop=True)
                else:
                    mm = pe.matmul(dst[:, 0:D], ones9[:, :], mix[:, 0:D], start=True, stop=True)
                mm.then_inc(coef_ps, 1)

            def split_matmul(dst, lhsT, rhs):
                for i, (k, rows, part) in enumerate(PARTS):
                    mm = pe.matmul(dst, lhsT(k, rows, part), rhs(k, rows, part), start=(i == 0),
                                   stop=(i == len(PARTS) - 1))
                return mm

            def step(t):
                if is_row(t, 0):
                    b = t
                    pe.wait_ge(x1T_done, b + 1)
                    x1_chunk = lambda k, rows, part: x1T[0:rows, k * T:(k + 1) * T]
                    split_matmul(ps_v[:, 0:D], x1_chunk, lambda k, rows, part:
                                 wqkv[part][0:rows, (3 * k + 2) * D:(3 * k + 3) * D]).then_inc(v_ps, 1)
                    if later(t, 0):
                        pe.wait_ge(qkT_done, b)
                    split_matmul(ps_qk[:, 0:2 * D], x1_chunk, lambda k, rows, part:
                                 wqkv[part][0:rows, 3 * k * D:(3 * k + 2) * D]).then_inc(qk_ps, 1)
                if is_row(t, LAG_S):
                    b = t - LAG_S
                    pe.wait_ge(qkT_done, b + 1)
                    if later(t, LAG_S):
                        pe.wait_ge(pT_done, b)
                    for c in range(2):
                        for j in range(HPB):
                            pe.matmul(s_bank[j][:, c * T:(c + 1) * T], ident_b[:, :], causal[:, :],
                                      start=True, stop=False)
                        for j in range(HPB):
                            part = slice(j * HD, (j + 1) * HD)
                            mm = pe.matmul(s_bank[j][:, c * T:(c + 1) * T], qkT[part, c * T:(c + 1) * T],
                                           qkT[part, (2 + c) * T:(3 + c) * T], start=False,
                                           stop=True)
                    mm.then_inc(s_ps, 1)
                if is_row(t, LAG_OW):
                    b = t - LAG_OW
                    pe.wait_ge(oT_done, b + 1)
                    if later(t, LAG_X2):
                        pe.wait_ge(x2T_done, b - 1)
                    elif later(t, LAG_OW):
                        pe.wait_ge(h1_done, b)
                    for c in range(2):
                        mm = pe.matmul(ps_ow[:, 0:D], oT[:, c * T:(c + 1) * T], wo_sb[:, c * D:(c + 1) * D],
                                       start=(c == 0), stop=(c == 1))
                    mm.then_inc(ow_ps, 1)
                if is_row(t, LAG_PV):
                    b = t - LAG_PV
                    pe.wait_ge(pT_done, b + 1)
                    pe.wait_ge(v_done, b + 1)
                    if later(t, LAG_PV):
                        pe.wait_ge(oT_done, b)
                    for h in range(HEADS):
                        s = 2 * (h % HPB) + h // HPB
                        mm = pe.matmul(ps_pv[:, h * VW:(h + 1) * VW], pT[:, s * T:(s + 1) * T],
                                       vaug[:, bass.ds(b * (HEADS * VW) + h * VW, VW)], start=True, stop=True,
                                       skip_group_check=True)
                    mm.then_inc(pv_ps, 1)
                if is_row(t, 0):
                    b = t
                    pe.wait_ge(qk_done, b + 1)
                    for c in range(4):
                        mm = pe.transpose(ps_qk[0:KH, c * T:(c + 1) * T], qk[:, c * KH:(c + 1) * KH], ident[:, :])
                    mm.then_inc(qkT_ps, 1)
                if is_row(t, -LEAD_LN1):
                    b = t + LEAD_LN1
                    pe.wait_ge(x1_done, b + 1)
                    if later(t, -LEAD_LN1):
                        pe.wait_ge(v_done, b)
                    for k in range(KC):
                        mm = pe.transpose(ps_v[:, k * T:(k + 1) * T], x1_parts[:, k * 128:(k + 1) * 128],
                                          ident[:, :])
                    mm.then_inc(x1T_ps, 1)
                if is_row(t, LAG_PV):
                    b = t - LAG_PV
                    pe.wait_ge(o_done, b + 1)
                    for c in range(2):
                        mm = pe.transpose(ps_pv[0:KH, c * T:(c + 1) * T], o[:, c * KH:(c + 1) * KH], ident[:, :])
                    mm.then_inc(oT_ps, 1)
                if is_row(t, LAG_X2):
                    b = t - LAG_X2
                    pe.wait_ge(x2_done, b + 1)
                    if not isinstance(b, int) or b + 1 < B:
                        pe.wait_ge(h1_done, b + 2)
                    else:
                        pe.wait_ge(x2T_done, b)
                    for k in range(KC):
                        mm = pe.transpose(ps_ow[:, k * T:(k + 1) * T], x2_parts[:, k * 128:(k + 1) * 128],
                                          ident[:, :])
                    mm.then_inc(x2T_ps, 1)
                if is_row(t, LAG_S):
                    b = t - LAG_S
                    pe.wait_ge(p_done, b + 1)
                    for h in range(HEADS):
                        mm = pe.transpose(s_bank[h // 2][:, (h % 2) * T:(h % 2 + 1) * T],
                                          p[:, h * T:(h + 1) * T], ident[:, :])
                    mm.then_inc(pT_ps, 1)

            def hidden(g, m, n):
                if not isinstance(n, int) or n >= 3:
                    pe.wait_ge(h_done, n - 2)
                split_matmul(ps_h[m % 3][:, :],
                             lambda k, rows, part: w0_part[part][0:rows, k * HID + m * 128:k * HID + (m + 1) * 128],
                             lambda k, rows, part: x2T[0:rows, bass.ds(g * GT + k * (B * T), GT)])\
                    .then_inc(h_ps, 1)

            def result(g, m, rows=range(GROUP)):
                for r in rows:
                    if m == 0 and later(g, 0):
                        pe.wait_ge(y_done, (g - 1) * GROUP + r + 1)
                    w = slice(m * GT + r * T, m * GT + (r + 1) * T)
                    pe.matmul(ps_y[r][:, 0:2 * D], hT["hi"][:, w], w1_parts[:, 2 * m * D:(2 * m + 2) * D],
                              start=(m == 0), stop=(m == HC - 1), skip_group_check=True)
                    mm = pe.matmul(ps_y[r][:, 0:D], hT["lo"][:, w], w1_parts[:, 2 * m * D:(2 * m + 1) * D],
                                   start=False, stop=(m == HC - 1), skip_group_check=True)
                return mm

            def between(t):
                for n in COEF_STEPS.get(t, ()):
                    coefficients(n)
                if t == -2:
                    pe.wait_ge(wqkv_hi, 2 * KC)
                    pe.wait_ge(wqkv_lo, 4)
                if t == LAG_OW - 1:
                    pe.wait_ge(coef_done, NCOEF)
                if t == HID_STEP:
                    pe.wait_ge(pT_done, B)
                    pe.wait_ge(w_hi, N0 + HC)
                    pe.wait_ge(w_lo, 4 + HC)
                for m in first_chunks(t):
                    hidden(0, m, m)

            pipeline(pe, step, between)

            pe.wait_ge(x2T_done, B)

            def overlapped(g):
                hidden(g + 1, 0, (g + 1) * HC)
                for m in range(HC):
                    if m + 1 < HC:
                        hidden(g + 1, m + 1, (g + 1) * HC + m + 1)
                    pe.wait_ge(h_split, g * HC + m + 1)
                    result(g, m).then_inc(h_used, 1)

            overlapped(0)
            with pe.Fori(1, NG - 1) as g:
                overlapped(g)
            for r in range(GROUP):
                for m in range(HC):
                    if r == 0:
                        pe.wait_ge(h_split, (NG - 1) * HC + m + 1)
                    mm = result(NG - 1, m, [r])
                mm.then_inc(row_ps, 1)


def kernel(**inputs):
    import numpy as np
    import concourse.bacc as bacc
    from concourse.bass_utils import run_bass_kernel_spmd

    a = {k: np.asarray(v) for k, v in inputs.items()}
    t = lambda k: a[k].T
    f = np.float32
    inv = f(1.0) / np.power(f(10000.0), np.arange(0, HD, 2, dtype=f) / f(HD))
    angle = np.outer(np.arange(T, dtype=f), inv).astype(f)
    cos, sin = np.cos(angle).astype(f), np.sin(angle).astype(f)
    arrays = {
        "ids_seg": np.concatenate([t("x"), t("mask_BS_i1_0")], axis=1),
        "tok_table": a["L0_tok_tok_table"],
        "rows_in": np.concatenate([a["L0_tok_seg_table"].reshape(-1), a["L0_tok_gamma"], a["L0_tok_beta"],
                                   a["L0_ffn_b_proj"]]),
        "pos_rope": np.concatenate([a["L0_tok_pos_table"][:T], cos, cos, -sin, sin], axis=1),
        "qkv_low_rank": np.concatenate([t(f"L0_attn_{w}A") for w in "qqkkvv"]
                                       + [a[f"L0_attn_{w}B"] for w in "qkv"], axis=1),
        "o_w": a["L0_attn_o_w"],
        "w_fc": np.concatenate([t("L0_ffn_w_fc")] * 2, axis=0),
        "b_fc": a["L0_ffn_b_fc"].reshape(HC, 128).T,
        "w_proj": t("L0_ffn_w_proj"),
        "mixing": np.concatenate([
            np.array([[d % D < e for d in range(2 * D)] for e in EMBEDS for _ in RATIOS], dtype=f),
            np.array([[h < r * e for h in range(HID)] for e in EMBEDS for r in RATIOS], dtype=f),
            np.repeat(a["L0_ffn_alpha_e"], len(RATIOS))[:, None],
            np.tile(a["L0_ffn_alpha_r"], len(EMBEDS))[:, None]], axis=1),
    }
    arrays = {k: np.ascontiguousarray(v) for k, v in arrays.items()}
    nc = bacc.Bacc("TRN2", target_bir_lowering=False, num_devices=1)
    args = [nc.dram_tensor(f"in_{k}", v.shape, mybir.dt.from_np(v.dtype), kind="ExternalInput").ap()
            for k, v in arrays.items()]
    out = nc.dram_tensor("out_0", (B, T, D), mybir.dt.float32, kind="ExternalOutput").ap()
    lm_layer(nc, *args, out)
    r = run_bass_kernel_spmd(nc, [{f"in_{k}": v for k, v in arrays.items()}], core_ids=[0])
    return r.results[0]["out_0"]
```

```python
import concourse.bass as bass
from concourse import mybir
from contextlib import ExitStack

B, T, D = 16, 128, 192
HEADS, HD = 6, 32
RANK = 48
HID = 768
KH = D // 2
KC = 2 * D // 128
PARTS = [(k, 128, "hi") for k in range(KC)] + [(0, 128, "lo"), (1, D - 128, "lo")]
HPB = HEADS // 2
PB = 512
VW = HD + 1
GROUP = 4
NG = B // GROUP
GT = GROUP * T
HC = HID // 128
EPS = 1e-5
MASKED = -1e30
SCALE = float(HD) ** -0.5
EMBEDS, RATIOS = (96, 144, 192), (2, 3, 4)
NC9 = len(EMBEDS) * len(RATIOS)

LAG_S, LAG_PV, LAG_OW, LAG_X2 = 1, 2, 3, 4
LEAD_EMB, LEAD_ST0, LEAD_LN0, LEAD_LN1 = 4, 3, 2, 1
FIRST, LAST = -LEAD_EMB, B - 1 + LAG_X2
N0 = 2 * KC
NCOEF = N0 + HC + 1
AHEAD = 4
EARLY = 0
EARLY_COEFS = 8
COEF_STEPS = {-1: range(8, 10), 0: range(10, 12), 1: range(12, NCOEF)}
SPLIT_STEPS = {0: range(0, 2), 1: range(2, 4), 2: range(4, N0), 3: range(N0, N0 + 3),
               4: range(N0 + 3, N0 + 5), B - LEAD_EMB: range(N0 + 5, NCOEF)}
STEADY = (LAG_X2 + 1, B - LEAD_EMB)
DRAIN = B + LAG_S
HID_PE = {"inside": {DRAIN - 1: range(0, 1), DRAIN: range(2, 3)},
          "behind": {DRAIN - 1: range(1, 2), DRAIN + 1: range(3, 5), DRAIN + 2: range(5, HC)}}
HID_ACT = {DRAIN: range(0, 1), DRAIN + 1: range(1, 3), DRAIN + 2: range(3, HC)}
HID_DVE = {DRAIN + 1: range(0, 1), DRAIN + 2: range(1, HC)}


def lm_layer(nc, ids_seg, tok_table, rows_in, pos_rope, qkv_low_rank, o_w, w_fc, b_fc, w_proj, mixing, out):
    fp32, bf16, f32r = mybir.dt.float32, mybir.dt.bfloat16, mybir.dt.float32r
    ALU, ACT, AX = mybir.AluOpType, mybir.ActivationFunctionType, mybir.AxisListType
    ctx = ExitStack()
    with ctx:
        def sb(name, shape, dt=fp32):
            return ctx.enter_context(nc.sbuf_tensor(name, shape, dt))

        def sem(name):
            return ctx.enter_context(nc.semaphore(name))

        ids_seg_sb = sb("ids_seg_sb", [T, 2 * B], mybir.dt.int32)
        ids_sb, seg_i = ids_seg_sb[:, 0:B], ids_seg_sb[:, B:2 * B]
        seg_f = sb("seg_f", [T, B])
        rows_sb = sb("rows_sb", [T, 5 * D])
        seg_rows, gamma_sb, beta_sb = rows_sb[:, 0:2 * D], rows_sb[:, 2 * D:3 * D], rows_sb[:, 3 * D:4 * D]
        bproj_sb = rows_sb[:, 4 * D:5 * D]
        seg_diff = sb("seg_diff", [T, D])
        pos_rope_sb = sb("pos_rope_sb", [T, D + 4 * HD])
        pos_sb, cos_sb = pos_rope_sb[:, 0:D], pos_rope_sb[:, D:D + 2 * HD]
        sin_sb = pos_rope_sb[:, D + 2 * HD:D + 4 * HD]
        proj_sb = sb("proj_sb", [RANK, 3 * 2 * D + 3 * D])
        projA, projB = proj_sb[:, 0:3 * 2 * D], proj_sb[:, 3 * 2 * D:3 * 3 * D]
        wqkv = {"hi": sb("wqkv_hi", [128, KC * 3 * D], f32r), "lo": sb("wqkv_lo", [128, 2 * 3 * D], f32r)}
        wo_sb = sb("wo_sb", [KH, 2 * D])
        w0 = sb("w0", [128, KC * HID])
        w0_part = {"hi": sb("w0_hi", [128, KC * HID], f32r), "lo": sb("w0_lo", [128, 2 * HID], f32r)}
        w1 = sb("w1", [128, HC * D])
        w1_parts = sb("w1_parts", [128, HC * 2 * D], f32r)
        bfc_sb = sb("bfc_sb", [128, HC])
        b0 = sb("b0", [128, HC])
        b1 = sb("b1", [T, D])
        mixing_sb = sb("mixing_sb", [NC9, 2 * D + HID + 2])
        m_in_sb, m_out_sb = mixing_sb[:, 0:2 * D], mixing_sb[:, 2 * D:2 * D + HID]
        alphas = mixing_sb[:, 2 * D + HID:]
        mix = sb("mix", [NC9, 2 * D + 2])
        mix_part = {"hi": sb("mix_hi", [NC9, 2 * D + 2], f32r), "lo": sb("mix_lo", [NC9, 2 * D + 2], f32r)}
        m_out_r = sb("m_out_r", [NC9, HID], f32r)
        ones9 = sb("ones9", [NC9, T])
        ones_r = sb("ones_r", [NC9, T], f32r)
        coef0 = sb("coef0", [128, KC * HID])
        coef1 = sb("coef1", [128, HC * (D + 1)])
        coef_b = sb("coef_b", [T, D])
        ident = sb("ident", [128, 128])
        ident_b = sb("ident_b", [128, 128], bf16)
        causal = sb("causal", [128, T], bf16)
        half_neg = sb("half_neg", [T, 1])
        eps_sb = sb("eps_sb", [T, 1])

        H = sb("H", [T, B * D])
        seg_add = sb("seg_add", [T, D])
        emb_sum = sb("emb_sum", [T, D])
        bn = [sb(f"bn{k}", [T, 6]) for k in range(3)]
        mv = [sb(f"mv{k}", [T, 2]) for k in range(3)]
        ve = [sb(f"ve{k}", [T, 1]) for k in range(3)]
        rstd = [sb(f"rstd{k}", [T, 1]) for k in range(3)]
        x1 = sb("x1", [T, D])
        x1_parts = sb("x1_parts", [T, 2 * D])
        x1T = sb("x1T", [128, KC * T], f32r)
        cos_part = sb("cos_part", [T, 2 * D])
        sin_part = sb("sin_part", [T, 2 * D])
        qk = sb("qk", [T, 2 * D])
        qkT = sb("qkT", [KH, 4 * T])
        vaug = sb("vaug", [T, B * HEADS * VW])
        nmax = sb("nmax", [T, HEADS])
        p = sb("p", [T, HEADS * T])
        pT = sb("pT", [T, HEADS * T])
        rsum = sb("rsum", [T, HEADS])
        o = sb("o", [T, D])
        oT = sb("oT", [KH, 2 * T])
        x2 = sb("x2", [T, D])
        x2_parts = sb("x2_parts", [T, 2 * D])
        x2T = sb("x2T", [128, KC * B * T], f32r)
        h_act = [sb(f"h_act{k}", [128, GT]) for k in range(3)]
        hT = {"hi": sb("hT_hi", [128, HC * GT], f32r), "lo": sb("hT_lo", [128, HC * GT], f32r)}

        def pb(name, banks=1):
            return ctx.enter_context(nc.psum_tensor(name, [128, banks * PB], fp32))

        ps_qkv = pb("ps_qkv", 2)
        ps_qk, ps_v = ps_qkv[:, 0:PB], ps_qkv[:, PB:2 * PB]
        QKV = 3 * D // 2
        qkv = ps_qkv[:, PB - QKV:PB + QKV]
        ps_pv, ps_ow, ps_x = (pb(f"ps_{n}")[:, :] for n in ("pv", "ow", "x"))
        ps_s = pb("ps_s", HPB)
        s_bank = [ps_s[:, j * PB:(j + 1) * PB] for j in range(HPB)]
        s_all = ps_s[:, :].rearrange("p (j n) -> p j n", j=HPB)[:, :, 0:2 * T]
        ps_w = [ps_qk, ps_v, *s_bank, ps_pv]
        ps_c = [ps_ow, ps_x]
        ps_h = [ps_x, ps_qk, ps_v]
        ps_y = [*s_bank, ps_pv]

        ids_in = sem("ids_in")
        emb_in = sem("emb_in")
        attn_in = sem("attn_in")
        mixing_in = sem("mixing_in")
        ffn_in = sem("ffn_in")
        tok_in = [sem(f"tok_in{b}") for b in range(B)]
        tok_rows = sem("tok_rows")
        pool_c = sem("pool_c")
        consts_done = sem("consts_done")
        seg_done = sem("seg_done")
        wqkv_ps = sem("wqkv_ps")
        wqkv_hi = sem("wqkv_hi")
        wqkv_lo = sem("wqkv_lo")
        w_hi = sem("w_hi")
        w_lo = sem("w_lo")
        mix_done = sem("mix_done")
        mix_hi = sem("mix_hi")
        mix_lo = sem("mix_lo")
        coef_ps = sem("coef_ps")
        coef_done = sem("coef_done")
        mixed = sem("mixed")
        emb_done = sem("emb_done")
        stats = [sem(f"stats{k}") for k in range(3)]
        rstd_done = [sem(f"rstd_done{k}") for k in range(3)]
        ve_done = [sem(f"ve_done{k}") for k in range(3)]
        bn_done = [sem(f"bn_done{k}") for k in range(3)]
        seg_added = sem("seg_added")
        emb_summed = sem("emb_summed")
        scaled = sem("scaled")
        h1_done = sem("h1_done")
        rope_parts = sem("rope_parts")
        rsum_done = sem("rsum_done")
        norm0_done = sem("norm0_done")
        h0_done = sem("h0_done")
        x1_norm = sem("x1_norm")
        x1_hi = sem("x1_hi")
        x1_done = sem("x1_done")
        x1T_ps = sem("x1T_ps")
        x1T_done = sem("x1T_done")
        qkv_ps = sem("qkv_ps")
        v_done = sem("v_done")
        qk_done = sem("qk_done")
        qkT_ps = sem("qkT_ps")
        qkT_done = sem("qkT_done")
        s_ps = sem("s_ps")
        max_done = sem("max_done")
        p_done = sem("p_done")
        pT_ps = sem("pT_ps")
        pT_done = sem("pT_done")
        pv_ps = sem("pv_ps")
        o_done = sem("o_done")
        oT_ps = sem("oT_ps")
        oT_done = sem("oT_done")
        ow_ps = sem("ow_ps")
        x2_norm = sem("x2_norm")
        x2_hi = sem("x2_hi")
        x2_done = sem("x2_done")
        x2T_ps = sem("x2T_ps")
        x2T_done = sem("x2T_done")
        res_done = sem("res_done")
        h_ps = sem("h_ps")
        h_done = sem("h_done")
        h_hi = sem("h_hi")
        h_split = sem("h_split")
        h_used = sem("h_used")
        row_ps = sem("row_ps")
        half_added = sem("half_added")
        y_done = sem("y_done")
        stored = sem("stored")

        block = ctx.enter_context(nc.Block())

        def row(t, b):
            return t[:, bass.ts(b, D)]

        def pipeline(eng, step, after=None):
            for t in range(FIRST, STEADY[0]):
                step(t)
                if after:
                    after(t)
            with eng.Fori(STEADY[0], STEADY[1]) as t:
                step(t)
            for t in range(STEADY[1], LAST + 1):
                step(t)
                if after:
                    after(t)

        def wait_apart(eng, sem, count):
            if not isinstance(count, int):
                eng.wait_ge(sem, 1)
            eng.wait_ge(sem, count)

        def is_row(t, d):
            return not isinstance(t, int) or 0 <= t - d < B

        def later(t, d=0):
            return not isinstance(t, int) or t - d >= 1

        def early(t):
            return isinstance(t, int) and t < EARLY

        def embed(eng, b):
            eng.tensor_tensor(seg_add[:, :], seg_diff[:, :],
                              seg_f[:, bass.ds(b, 1)].to_broadcast([T, D]), ALU.mult).then_inc(seg_added, 1)
            wait_apart(eng, seg_added, b + 1)
            eng.tensor_tensor(emb_sum[:, :], seg_add[:, :], pos_sb, ALU.add).then_inc(emb_summed, 1)
            wait_apart(eng, emb_summed, b + 1)
            eng.wait_ge(tok_rows, b + 1)
            eng.tensor_tensor(row(H, b), row(H, b), emb_sum[:, :], ALU.add).then_inc(emb_done, 1)

        def scale_shift(eng, b):
            wait_apart(eng, norm0_done, b + 1)
            eng.tensor_tensor(row(H, b), row(H, b), gamma_sb, ALU.mult).then_inc(scaled, 1)
            wait_apart(eng, scaled, b + 1)
            eng.tensor_tensor(row(H, b), row(H, b), beta_sb, ALU.add).then_inc(h0_done, 1)

        def chunk0(k, half):
            return slice(k * HID + half * HID // 2, k * HID + (half + 1) * HID // 2)

        @block.sync
        def _(sp):
            sp.dma_start(ids_seg_sb[:, :], ids_seg).then_inc(ids_in, 16)
            sp.dma_start(rows_sb[:, :], rows_in.partition_broadcast(T)).then_inc(emb_in, 16)
            sp.dma_start(mixing_sb[:, :], mixing).then_inc(mixing_in, 16)
            for b in range(B):
                sp.wait_ge(tok_in[b], 16)
                sp.sem_inc(tok_rows, 1)
                if b == AHEAD - 1:
                    sp.dma_start(w0[:, :].rearrange("p (k n) -> p k n", k=KC),
                                 w_fc.rearrange("(k p) n -> p k n", p=128)).then_inc(ffn_in, 16)
                    sp.dma_start(w1[:, :].rearrange("p (c n) -> p c n", c=HC),
                                 w_proj.rearrange("(c p) n -> p c n", p=128)).then_inc(ffn_in, 16)
                    sp.dma_start(bfc_sb[:, :], b_fc).then_inc(ffn_in, 16)
            with sp.Fori(0, NG - 1) as g:
                sp.wait_ge(y_done, g * GROUP + GROUP)
                sp.dma_start(out[bass.ts(g, GROUP), :, :].rearrange("b t d -> t b d"),
                             H[:, bass.ts(g, GROUP * D)].rearrange("t (b d) -> t b d", d=D))\
                  .then_inc(stored, 16)
            for b in range(B - GROUP, B):
                sp.wait_ge(y_done, b + 1)
                sp.dma_start(out[b, :, :], row(H, b)).then_inc(stored, 16)
            sp.wait_ge(stored, 16 * (NG - 1 + GROUP))

        @block.gpsimd
        def _(pool):
            pool.wait_ge(ids_in, 16)

            def gather(b):
                pool.indirect_dma_start(out=row(H, b), out_offset=None, in_=tok_table,
                                        in_offset=bass.IndirectOffsetOnAxis(ap=ids_sb[:, b:b + 1], axis=0))\
                    .then_inc(tok_in[b], 16)

            for b in range(AHEAD):
                gather(b)
            pool.memset(ident[:, :], 0.0).then_inc(pool_c, 1)
            pool.memset(ident_b[:, :], 0.0).then_inc(pool_c, 1)
            pool.memset(causal[:, :], 0.0).then_inc(pool_c, 1)
            pool.memset(vaug[:, :].rearrange("p (n e) -> p n e", e=VW)[:, :, HD:VW], 1.0).then_inc(pool_c, 1)
            pool.memset(half_neg[:, :], -0.5).then_inc(pool_c, 1)
            pool.memset(eps_sb[:, :], EPS).then_inc(pool_c, 1)
            pool.memset(ones9[:, :], 1.0).then_inc(pool_c, 1)
            pool.wait_ge(pool_c, 7)
            for m in (ident, ident_b):
                pool.affine_select(out=m[:, :], in_=m[:, :], compare_op=ALU.not_equal, fill=1.0, base=0,
                                   pattern=[[-1, 128]], channel_multiplier=1).then_inc(consts_done, 1)
            pool.affine_select(out=causal[:, :], in_=causal[:, :], compare_op=ALU.is_ge, fill=MASKED, base=0,
                               pattern=[[-1, T]], channel_multiplier=1).then_inc(consts_done, 1)

            def inv_std(k, b):
                wait_apart(pool, stats[k], b + 1)
                pool.tensor_tensor(ve[k][:, :], mv[k][:, 1:2], eps_sb[:, :], ALU.add).then_inc(ve_done[k], 1)
                pool.wait_ge(ve_done[k], b + 1)
                pool.tensor_tensor(rstd[k][:, :], ve[k][:, :], half_neg[:, :], ALU.pow)\
                    .then_inc(rstd_done[k], 1)

            def step(t):
                if is_row(t, -LEAD_LN0) and not early(t):
                    scale_shift(pool, t + LEAD_LN0)
                if is_row(t, -LEAD_ST0):
                    inv_std(0, t + LEAD_ST0)
                if is_row(t, -LEAD_EMB) and not early(t):
                    if isinstance(t, int) and t == EARLY:
                        pool.wait_ge(emb_done, t + LEAD_EMB)
                    embed(pool, t + LEAD_EMB)
                if is_row(t, LAG_OW):
                    inv_std(2, t - LAG_OW)
                if is_row(t, -LEAD_LN0):
                    inv_std(1, t + LEAD_LN0)

            def between(t):
                begin = AHEAD + (t - FIRST if t < 0 else -FIRST + 2 * t)
                for b in range(begin, min(begin + (1 if t < 0 else 2), B)):
                    gather(b)
                for n in SPLIT_STEPS.get(t, ()):
                    if n < N0 + HC:
                        pool.wait_ge(w_hi, n + 1)
                    if n < 4:
                        w, rows = chunk0(n // 2, n % 2), 128 if n < 2 else D - 128
                        pool.tensor_tensor(w0_part["lo"][0:rows, w], w0[0:rows, w],
                                           w0_part["hi"][0:rows, w].bitcast(fp32), ALU.subtract).then_inc(w_lo, 1)
                    elif N0 <= n < N0 + HC:
                        m = n - N0
                        pool.tensor_tensor(w1_parts[:, (2 * m + 1) * D:(2 * m + 2) * D], w1[:, m * D:(m + 1) * D],
                                           w1_parts[:, 2 * m * D:(2 * m + 1) * D].bitcast(fp32), ALU.subtract)\
                            .then_inc(w_lo, 1)

            pipeline(pool, step, between)

            pool.wait_ge(mixed, NCOEF)
            with pool.Fori(0, NG) as g:
                wait_apart(pool, x2_done, g * GROUP + GROUP)
                rows = H[:, bass.ts(g, GROUP * D)].rearrange("t (b d) -> t b d", d=D)
                pool.tensor_tensor(rows, rows, b1[:, :].unsqueeze(1).to_broadcast([T, GROUP, D]), ALU.add)\
                    .then_inc(res_done, 1)

        @block.scalar
        def _(act):
            act.dma_start(pos_rope_sb[:, :], pos_rope).then_inc(emb_in, 16)
            act.dma_start(proj_sb[:, :], qkv_low_rank).then_inc(attn_in, 16)
            act.dma_start(wo_sb[:, :].rearrange("p (c n) -> p c n", c=2),
                          o_w.rearrange("(c p) n -> p c n", p=KH)).then_inc(attn_in, 16)
            act.wait_ge(mix_done, 2)
            act.copy(mix_part["hi"][:, :], mix[:, :]).then_inc(mix_hi, 1)
            act.copy(m_out_r[:, :], m_out_sb).then_inc(mix_hi, 1)
            act.wait_ge(pool_c, 7)
            act.copy(ones_r[:, :], ones9[:, :]).then_inc(mix_hi, 1)
            for n in range(2 * KC):
                w = slice(n // 2 * 3 * D + n % 2 * 2 * D, n // 2 * 3 * D + (2 + n % 2) * D)
                act.wait_ge(wqkv_ps, n + 1)
                act.copy(wqkv["hi"][:, w], ps_w[n][:, 0:(2 - n % 2) * D]).then_inc(wqkv_hi, 1)

            def coefficients_out(n):
                act.wait_ge(coef_ps, n + 1)
                if n < N0:
                    dst, w = coef0[:, chunk0(n // 2, n % 2)], HID // 2
                elif n < N0 + HC:
                    dst, w = coef1[:, (n - N0) * (D + 1):(n - N0 + 1) * (D + 1)], D + 1
                else:
                    dst, w = coef_b[:, :], D
                act.copy(dst, ps_c[n % 2][:, 0:w]).then_inc(coef_done, 1)

            for n in range(EARLY_COEFS):
                coefficients_out(n)

            def high_part(dst, x):
                return act.copy(dst[:, 0:D].bitcast(f32r), x[:, :])

            def exponentials(slots):
                for h in slots:
                    e = act.activation(p[:, h * T:(h + 1) * T], s_bank[h // 2][:, (h % 2) * T:(h % 2 + 1) * T],
                                       ACT.Exp, bias=nmax[:, h:h + 1])
                return e

            def step(t):
                if is_row(t, LAG_X2):
                    b = t - LAG_X2
                    act.wait_ge(x2_norm, b + 1)
                    if later(t, LAG_X2):
                        act.wait_ge(x2T_ps, b)
                    high_part(x2_parts, x2).then_inc(x2_hi, 1)
                if is_row(t, -LEAD_LN1):
                    b = t + LEAD_LN1
                    act.wait_ge(x1_norm, b + 1)
                    if later(t, -LEAD_LN1):
                        act.wait_ge(x1T_ps, b)
                    high_part(x1_parts, x1).then_inc(x1_hi, 1)
                if isinstance(t, int):
                    for n in COEF_STEPS.get(t - 1, ()):
                        coefficients_out(n)
                if is_row(t, 0):
                    b = t
                    act.wait_ge(qkv_ps, 2 * b + 2)
                    act.wait_ge(rope_parts, 3 * b + 3)
                    act.copy(vaug[:, bass.ts(b, HEADS * VW)].rearrange("p (h e) -> p h e", e=VW)[:, :, 0:HD],
                             qkv[:, 2 * D:3 * D].rearrange("p (h e) -> p h e", e=HD)).then_inc(v_done, 1)
                if is_row(t, LAG_S):
                    b = t - LAG_S
                    act.wait_ge(max_done, b + 1)
                    if later(t, LAG_S):
                        act.wait_ge(pT_ps, b)
                    exponentials(range(0, 4)).then_inc(p_done, 1)
                if is_row(t, LAG_S):
                    exponentials(range(4, HEADS)).then_inc(p_done, 1)
                if is_row(t, -LEAD_LN1):
                    b = t + LEAD_LN1
                    act.wait_ge(x1T_ps, b + 1)
                    if later(t, -LEAD_LN1):
                        act.wait_ge(qkv_ps, 2 * b)
                    act.copy(x1T[:, :], ps_v[:, 0:KC * T]).then_inc(x1T_done, 1)
                if is_row(t, 0):
                    b = t
                    act.wait_ge(qkT_ps, b + 1)
                    if later(t):
                        act.wait_ge(s_ps, b)
                    act.copy(qkT[:, :], ps_qk[0:KH, 0:4 * T]).then_inc(qkT_done, 1)
                if is_row(t, LAG_S):
                    b = t - LAG_S
                    act.wait_ge(pT_ps, b + 1)
                    if later(t, LAG_S):
                        act.wait_ge(pv_ps, b)
                    act.copy(pT[:, :].rearrange("p (j n) -> p j n", j=HPB), s_all).then_inc(pT_done, 1)
                if is_row(t, LAG_PV):
                    b = t - LAG_PV
                    act.wait_ge(oT_ps, b + 1)
                    if later(t, LAG_PV):
                        act.wait_ge(ow_ps, b)
                    act.copy(oT[:, :], ps_pv[0:KH, 0:2 * T]).then_inc(oT_done, 1)
                if is_row(t, LAG_X2):
                    b = t - LAG_X2
                    act.wait_ge(x2T_ps, b + 1)
                    act.copy(x2T[:, :].rearrange("p (k n) -> p k n", k=KC)[:, :, bass.ts(b, T)],
                             ps_ow[:, 0:KC * T].rearrange("p (k n) -> p k n", k=KC)).then_inc(x2T_done, 1)

            def gelu(g, m):
                act.wait_ge(h_ps, g * HC + m + 1)
                if m >= 3 or later(g, 0):
                    act.wait_ge(h_split, g * HC + m - 2)
                act.activation(h_act[m % 3][:, :], ps_h[m % 3][:, :], ACT.Gelu_apprx_tanh,
                               bias=b0[:, m:m + 1]).then_inc(h_done, 1)

            def between(t):
                for n in SPLIT_STEPS.get(t, ()):
                    act.wait_ge(mixed, n + 1)
                    if n < N0:
                        w = chunk0(n // 2, n % 2)
                        act.copy(w0_part["hi"][:, w], w0[:, w]).then_inc(w_hi, 1)
                    elif n < N0 + HC:
                        m = n - N0
                        act.copy(w1_parts[:, 2 * m * D:(2 * m + 1) * D], w1[:, m * D:(m + 1) * D])\
                           .then_inc(w_hi, 1)
                for m in HID_ACT.get(t, ()):
                    gelu(0, m)

            pipeline(act, step, between)

            with act.Fori(1, NG) as g:
                for m in range(HC):
                    gelu(g, m)

        @block.vector
        def _(dve):
            dve.wait_ge(ids_in, 16)
            dve.wait_ge(emb_in, 2 * 16)
            dve.tensor_copy(seg_f[:, :], seg_i).then_inc(seg_done, 1)
            dve.tensor_tensor(pos_sb, pos_sb, seg_rows[:, 0:D], ALU.add).then_inc(seg_done, 1)
            dve.tensor_tensor(seg_diff[:, :], seg_rows[:, D:2 * D], seg_rows[:, 0:D], ALU.subtract)\
               .then_inc(seg_done, 1)
            dve.wait_ge(mixing_in, 16)
            dve.tensor_scalar(mix[:, 0:2 * D], m_in_sb, alphas[:, 0:1], alphas[:, 1:2],
                              ALU.mult, ALU.mult).then_inc(mix_done, 1)
            dve.tensor_tensor(mix[:, 2 * D:2 * D + 2], alphas[:, 0:1].to_broadcast([NC9, 2]),
                              alphas[:, 1:2].to_broadcast([NC9, 2]), ALU.mult).then_inc(mix_done, 1)
            dve.wait_ge(seg_done, 3)

            def layer_stats(k, b, x):
                dve.bn_stats(bn[k][:, :], x).then_inc(bn_done[k], 1)
                wait_apart(dve, bn_done[k], b + 1)
                dve.bn_aggr(mv[k][:, :], bn[k][:, :]).then_inc(stats[k], 1)

            def normalize(k, b, dst, x, done):
                dve.wait_ge(rstd_done[k], b + 1)
                dve.tensor_scalar(dst, x, mv[k][:, 0:1], rstd[k][:, 0:1], ALU.subtract, ALU.mult)\
                   .then_inc(done, 1)

            def low_part(dst, x, hi, b):
                dve.wait_ge(hi, b + 1)
                return dve.tensor_tensor(dst[:, D:2 * D].bitcast(f32r), x[:, :], dst[:, 0:D], ALU.subtract)

            def step(t):
                if is_row(t, -LEAD_LN0):
                    b = t + LEAD_LN0
                    normalize(0, b, row(H, b), row(H, b), norm0_done)
                    if early(t):
                        scale_shift(dve, b)
                if is_row(t, LAG_X2):
                    b = t - LAG_X2
                    normalize(2, b, x2[:, :], row(H, b), x2_norm)
                if is_row(t, -LEAD_LN1):
                    b = t + LEAD_LN1
                    normalize(1, b, x1[:, :], row(H, b), x1_norm)
                if is_row(t, -LEAD_EMB) and early(t):
                    embed(dve, t + LEAD_EMB)
                if is_row(t, -LEAD_ST0):
                    b = t + LEAD_ST0
                    wait_apart(dve, emb_done, b + 1)
                    if later(t, -LEAD_ST0):
                        dve.wait_ge(norm0_done, b)
                    layer_stats(0, b, row(H, b))
                if is_row(t, LAG_X2):
                    b = t - LAG_X2
                    low_part(x2_parts, x2, x2_hi, b).then_inc(x2_done, 1)
                if is_row(t, -LEAD_LN1):
                    b = t + LEAD_LN1
                    low_part(x1_parts, x1, x1_hi, b).then_inc(x1_done, 1)
                if is_row(t, 0):
                    b = t
                    half = HD // 2

                    def heads(x):
                        return x[:, 0:2 * D].rearrange("p (w h e) -> p w h e", w=2, e=HD)

                    def table(x, part):
                        t3 = x.rearrange("p (w e) -> p w e", w=2)[:, :, part]
                        return t3.unsqueeze(2).to_broadcast([T, 2, HEADS, part.stop - part.start])

                    first, second, whole = slice(0, half), slice(half, HD), slice(0, HD)
                    dve.wait_ge(qkv_ps, 2 * b + 2)
                    if later(t, 0):
                        dve.wait_ge(qk_done, b)
                    dve.tensor_tensor(heads(cos_part), heads(qkv), table(cos_sb, whole), ALU.mult)\
                       .then_inc(rope_parts, 1)
                    dve.tensor_tensor(heads(sin_part)[:, :, :, first], heads(qkv)[:, :, :, second],
                                      table(sin_sb, first), ALU.mult).then_inc(rope_parts, 1)
                    dve.tensor_tensor(heads(sin_part)[:, :, :, second], heads(qkv)[:, :, :, first],
                                      table(sin_sb, second), ALU.mult).then_inc(rope_parts, 1)
                    dve.wait_ge(rope_parts, 3 * b + 3)
                    if later(t, 0):
                        dve.wait_ge(qkT_ps, b)
                    dve.tensor_tensor(qk[:, :], cos_part[:, :], sin_part[:, :], ALU.add).then_inc(qk_done, 1)
                if is_row(t, LAG_S):
                    b = t - LAG_S
                    dve.wait_ge(s_ps, b + 1)
                    if later(t, LAG_S):
                        dve.wait_ge(p_done, 2 * b)
                    dve.tensor_reduce(nmax[:, :].rearrange("p (j c) -> p j c", c=2),
                                      s_all.rearrange("p j (c k) -> p j c k", k=T), AX.X, ALU.max,
                                      negate=True).then_inc(max_done, 1)
                if is_row(t, LAG_PV):
                    b = t - LAG_PV
                    pv3 = ps_pv[:, 0:HEADS * VW].rearrange("p (h e) -> p h e", e=VW)
                    dve.wait_ge(pv_ps, b + 1)
                    dve.reciprocal(rsum[:, :].unsqueeze(2), pv3[:, :, HD:VW]).then_inc(rsum_done, 1)
                    dve.wait_ge(rsum_done, b + 1)
                    if later(t, LAG_PV):
                        dve.wait_ge(oT_ps, b)
                    dve.tensor_tensor(o[:, :].rearrange("p (h e) -> p h e", e=HD), pv3[:, :, 0:HD],
                                      rsum[:, :].unsqueeze(2).to_broadcast([T, HEADS, HD]), ALU.mult)\
                       .then_inc(o_done, 1)
                if is_row(t, LAG_OW):
                    b = t - LAG_OW
                    dve.wait_ge(ow_ps, b + 1)
                    dve.tensor_tensor(row(H, b), row(H, b), ps_ow[:, 0:D], ALU.add).then_inc(h1_done, 1)
                    wait_apart(dve, h1_done, b + 1)
                    if later(t, LAG_OW):
                        dve.wait_ge(x2_norm, b)
                    layer_stats(2, b, row(H, b))
                if is_row(t, -LEAD_LN0):
                    b = t + LEAD_LN0
                    wait_apart(dve, h0_done, b + 1)
                    if later(t, -LEAD_LN0):
                        dve.wait_ge(x1_norm, b)
                    layer_stats(1, b, row(H, b))

            def mix_weights(n):
                dve.wait_ge(ffn_in, 3 * 16)
                dve.wait_ge(coef_done, n + 1)
                if n < N0:
                    w = chunk0(n // 2, n % 2)
                    dve.tensor_tensor(w0[:, w], w0[:, w], coef0[:, w], ALU.mult).then_inc(mixed, 1)
                elif n < N0 + HC:
                    m = n - N0
                    w, c = slice(m * D, (m + 1) * D), m * (D + 1)
                    dve.tensor_tensor(b0[:, m:m + 1], bfc_sb[:, m:m + 1], coef1[:, c + D:c + D + 1], ALU.mult)
                    dve.tensor_tensor(w1[:, w], w1[:, w], coef1[:, c:c + D], ALU.mult).then_inc(mixed, 1)
                else:
                    dve.tensor_tensor(b1[:, :], bproj_sb, coef_b[:, :], ALU.mult).then_inc(mixed, 1)

            def split_hidden(g, m):
                w, x = slice(m * GT, (m + 1) * GT), h_act[m % 3][:, :]
                dve.wait_ge(h_done, g * HC + m + 1)
                if later(g, 0):
                    dve.wait_ge(h_used, (g - 1) * HC + m + 1)
                dve.tensor_copy(hT["hi"][:, w], x).then_inc(h_hi, 1)
                dve.wait_ge(h_hi, g * HC + m + 1)
                dve.tensor_tensor(hT["lo"][:, w], x, hT["hi"][:, w].bitcast(fp32), ALU.subtract)\
                   .then_inc(h_split, 1)

            def fold_low_parts():
                dve.wait_ge(mix_hi, 3)
                dve.tensor_tensor(mix_part["lo"][:, :], mix[:, :], mix_part["hi"][:, :].bitcast(fp32),
                                  ALU.subtract).then_inc(mix_lo, 1)
                for n in range(4):
                    rows = slice(0, 128 if n < 2 else D - 128)
                    w = slice(n // 2 * 3 * D + n % 2 * 2 * D, n // 2 * 3 * D + (2 + n % 2) * D)
                    dve.wait_ge(wqkv_hi, n + 1)
                    dve.tensor_tensor(wqkv["lo"][rows, w], ps_w[n][rows, 0:(2 - n % 2) * D],
                                      wqkv["hi"][rows, w].bitcast(fp32), ALU.subtract).then_inc(wqkv_lo, 1)

            def between(t):
                if t == FIRST + 1:
                    fold_low_parts()
                for n in SPLIT_STEPS.get(t, ()):
                    mix_weights(n)
                for m in HID_DVE.get(t, ()):
                    split_hidden(0, m)

            pipeline(dve, step, between)

            def residual(g, r):
                x = row(H, g * GROUP + r)
                dve.tensor_tensor(x, x, ps_y[r][:, 0:D], ALU.add).then_inc(half_added, 1)
                dve.wait_ge(half_added, g * GROUP + r + 1)
                dve.tensor_tensor(x, x, ps_y[r][:, D:2 * D], ALU.add).then_inc(y_done, 1)

            with dve.Fori(0, NG - 1) as g:
                for m in range(HC - 1):
                    split_hidden(g + 1, m)
                dve.wait_ge(h_used, g * HC + HC)
                dve.wait_ge(res_done, g + 1)
                for r in range(GROUP):
                    residual(g, r)
                split_hidden(g + 1, HC - 1)
            dve.wait_ge(res_done, NG)
            for r in range(GROUP):
                dve.wait_ge(row_ps, r + 1)
                residual(NG - 1, r)

        @block.tensor
        def _(pe):
            pe.wait_ge(attn_in, 2 * 16)
            for n in range(2 * KC):
                k = n // 2
                for i, j in enumerate((0, 1) if n % 2 == 0 else (2,)):
                    mm = pe.matmul(ps_w[n][:, i * D:(i + 1) * D],
                                   projA[:, j * 2 * D + k * 128:j * 2 * D + (k + 1) * 128],
                                   projB[:, j * D:(j + 1) * D], start=True, stop=True)
                mm.then_inc(wqkv_ps, 1)

            def coefficients(n):
                if n >= 2:
                    pe.wait_ge(coef_done, n - 1)
                dst = ps_c[n % 2]
                for i, part in enumerate(("hi", "lo")):
                    x, ends = mix_part[part], dict(start=(i == 0), stop=(i == 1))
                    if n < N0:
                        k, half = n // 2, n % 2
                        mm = pe.matmul(dst[:, 0:HID // 2], x[:, k * 128:(k + 1) * 128],
                                       m_out_r[:, half * HID // 2:(half + 1) * HID // 2], **ends)
                    elif n < N0 + HC:
                        m = n - N0
                        mm = pe.matmul(dst[:, 0:D + 2], m_out_r[:, m * 128:(m + 1) * 128],
                                       x[:, D:2 * D + 2], **ends)
                    else:
                        mm = pe.matmul(dst[:, 0:D], ones_r[:, :], x[:, 0:D], **ends)
                mm.then_inc(coef_ps, 1)

            pe.wait_ge(mix_hi, 3)
            pe.wait_ge(mix_lo, 1)
            pe.wait_ge(consts_done, 3)
            for n in range(EARLY_COEFS):
                coefficients(n)
            pe.wait_ge(wqkv_hi, 2 * KC)
            pe.wait_ge(wqkv_lo, 4)

            def split_matmul(dst, lhsT, rhs):
                for i, (k, rows, part) in enumerate(PARTS):
                    mm = pe.matmul(dst, lhsT(k, rows, part), rhs(k, rows, part), start=(i == 0),
                                   stop=(i == len(PARTS) - 1))
                return mm

            def hidden(g, m, n):
                if not isinstance(n, int) or n >= 3:
                    pe.wait_ge(h_done, n - 2)
                weights = lambda k, rows, part: w0_part[part][0:rows, k * HID + m * 128:k * HID + (m + 1) * 128]
                tokens = lambda k, rows, part: x2T[0:rows, bass.ds(g * GT + k * (B * T), GT)]
                split_matmul(ps_h[m % 3][:, :], weights, tokens).then_inc(h_ps, 1)

            def step(t):
                if is_row(t, 0):
                    b = t
                    pe.wait_ge(x1T_done, b + 1)
                    x1_chunk = lambda k, rows, part: x1T[0:rows, k * T:(k + 1) * T]
                    if later(t, 0):
                        pe.wait_ge(qkT_done, b)
                    for i in range(2):
                        split_matmul(qkv[:, i * QKV:(i + 1) * QKV], x1_chunk, lambda k, rows, part:
                                     wqkv[part][0:rows, 3 * k * D + i * QKV:3 * k * D + (i + 1) * QKV])\
                            .then_inc(qkv_ps, 1)
                if is_row(t, LAG_S):
                    b = t - LAG_S
                    pe.wait_ge(qkT_done, b + 1)
                    if later(t, LAG_S):
                        pe.wait_ge(pT_done, b)
                    for c in range(2):
                        for j in range(HPB):
                            pe.matmul(s_bank[j][:, c * T:(c + 1) * T], ident_b[:, :], causal[:, :],
                                      start=True, stop=False)
                        for j in range(HPB):
                            part = slice(j * HD, (j + 1) * HD)
                            mm = pe.matmul(s_bank[j][:, c * T:(c + 1) * T], qkT[part, c * T:(c + 1) * T],
                                           qkT[part, (2 + c) * T:(3 + c) * T], start=False,
                                           stop=True)
                    mm.then_inc(s_ps, 1)
                if is_row(t, LAG_OW):
                    b = t - LAG_OW
                    pe.wait_ge(oT_done, b + 1)
                    if later(t, LAG_X2):
                        pe.wait_ge(x2T_done, b - 1)
                    elif later(t, LAG_OW):
                        pe.wait_ge(h1_done, b)
                    for c in range(2):
                        mm = pe.matmul(ps_ow[:, 0:D], oT[:, c * T:(c + 1) * T], wo_sb[:, c * D:(c + 1) * D],
                                       start=(c == 0), stop=(c == 1))
                    mm.then_inc(ow_ps, 1)
                if is_row(t, LAG_PV):
                    b = t - LAG_PV
                    pe.wait_ge(pT_done, b + 1)
                    pe.wait_ge(v_done, b + 1)
                    if later(t, LAG_PV):
                        pe.wait_ge(oT_done, b)
                    for h in range(HEADS):
                        s = 2 * (h % HPB) + h // HPB
                        mm = pe.matmul(ps_pv[:, h * VW:(h + 1) * VW], pT[:, s * T:(s + 1) * T],
                                       vaug[:, bass.ds(b * (HEADS * VW) + h * VW, VW)], start=True, stop=True,
                                       skip_group_check=True)
                    mm.then_inc(pv_ps, 1)
                if is_row(t, 0):
                    b = t
                    pe.wait_ge(qk_done, b + 1)
                    for c in range(4):
                        mm = pe.transpose(ps_qk[0:KH, c * T:(c + 1) * T], qk[:, c * KH:(c + 1) * KH], ident[:, :])
                    mm.then_inc(qkT_ps, 1)
                if is_row(t, -LEAD_LN1):
                    b = t + LEAD_LN1
                    pe.wait_ge(x1_done, b + 1)
                    if later(t, -LEAD_LN1):
                        pe.wait_ge(v_done, b)
                    for k in range(KC):
                        mm = pe.transpose(ps_v[:, k * T:(k + 1) * T], x1_parts[:, k * 128:(k + 1) * 128],
                                          ident[:, :])
                    mm.then_inc(x1T_ps, 1)
                if isinstance(t, int) and t in HID_PE["inside"]:
                    pe.wait_ge(w_hi, N0 + HC)
                    pe.wait_ge(w_lo, 4 + HC)
                    for m in HID_PE["inside"][t]:
                        hidden(0, m, m)
                if is_row(t, LAG_PV):
                    b = t - LAG_PV
                    pe.wait_ge(o_done, b + 1)
                    for c in range(2):
                        mm = pe.transpose(ps_pv[0:KH, c * T:(c + 1) * T], o[:, c * KH:(c + 1) * KH], ident[:, :])
                    mm.then_inc(oT_ps, 1)
                if is_row(t, LAG_X2):
                    b = t - LAG_X2
                    pe.wait_ge(x2_done, b + 1)
                    if not isinstance(b, int) or b + 1 < B:
                        pe.wait_ge(h1_done, b + 2)
                    else:
                        pe.wait_ge(x2T_done, b)
                    for k in range(KC):
                        mm = pe.transpose(ps_ow[:, k * T:(k + 1) * T], x2_parts[:, k * 128:(k + 1) * 128],
                                          ident[:, :])
                    mm.then_inc(x2T_ps, 1)
                if is_row(t, LAG_S):
                    b = t - LAG_S
                    for h in range(HEADS):
                        if h in (0, 4):
                            pe.wait_ge(p_done, 2 * b + 1 + h // 4)
                        mm = pe.transpose(s_bank[h // 2][:, (h % 2) * T:(h % 2 + 1) * T],
                                          p[:, h * T:(h + 1) * T], ident[:, :])
                    mm.then_inc(pT_ps, 1)

            def result(g, m, rows=range(GROUP)):
                for r in rows:
                    if m == 0 and later(g, 0):
                        pe.wait_ge(y_done, (g - 1) * GROUP + r + 1)
                    w = slice(m * GT + r * T, m * GT + (r + 1) * T)
                    pe.matmul(ps_y[r][:, 0:2 * D], hT["hi"][:, w], w1_parts[:, 2 * m * D:(2 * m + 2) * D],
                              start=(m == 0), stop=(m == HC - 1), skip_group_check=True)
                    mm = pe.matmul(ps_y[r][:, 0:D], hT["lo"][:, w], w1_parts[:, 2 * m * D:(2 * m + 1) * D],
                                   start=False, stop=(m == HC - 1), skip_group_check=True)
                return mm

            def between(t):
                for n in COEF_STEPS.get(t, ()):
                    coefficients(n)
                if t == LAG_OW - 1:
                    pe.wait_ge(coef_done, NCOEF)
                for m in HID_PE["behind"].get(t, ()):
                    hidden(0, m, m)

            pipeline(pe, step, between)

            pe.wait_ge(x2T_done, 2 * GROUP)

            def overlapped(g):
                hidden(g + 1, 0, (g + 1) * HC)
                for m in range(HC):
                    if m + 1 < HC:
                        hidden(g + 1, m + 1, (g + 1) * HC + m + 1)
                    pe.wait_ge(h_split, g * HC + m + 1)
                    result(g, m).then_inc(h_used, 1)

            overlapped(0)
            pe.wait_ge(x2T_done, B)
            with pe.Fori(1, NG - 1) as g:
                overlapped(g)
            for r in range(GROUP):
                for m in range(HC):
                    if r == 0:
                        pe.wait_ge(h_split, (NG - 1) * HC + m + 1)
                    mm = result(NG - 1, m, [r])
                mm.then_inc(row_ps, 1)


def kernel(**inputs):
    import numpy as np
    import concourse.bacc as bacc
    from concourse.bass_utils import run_bass_kernel_spmd

    a = {k: np.asarray(v) for k, v in inputs.items()}
    t = lambda k: a[k].T
    f = np.float32
    inv = f(1.0) / np.power(f(10000.0), np.arange(0, HD, 2, dtype=f) / f(HD))
    angle = np.outer(np.arange(T, dtype=f), inv).astype(f)
    scale = f(SCALE)
    cos, sin = np.cos(angle).astype(f), np.sin(angle).astype(f)
    arrays = {
        "ids_seg": np.concatenate([t("x"), t("mask_BS_i1_0")], axis=1),
        "tok_table": a["L0_tok_tok_table"],
        "rows_in": np.concatenate([a["L0_tok_seg_table"].reshape(-1), a["L0_tok_gamma"], a["L0_tok_beta"],
                                   a["L0_ffn_b_proj"]]),
        "pos_rope": np.concatenate([a["L0_tok_pos_table"][:T], cos * scale, cos * scale, cos, cos,
                                    -sin * scale, sin * scale, -sin, sin], axis=1),
        "qkv_low_rank": np.concatenate([t(f"L0_attn_{w}A") for w in "qqkkvv"]
                                       + [a[f"L0_attn_{w}B"] for w in "qkv"], axis=1),
        "o_w": a["L0_attn_o_w"],
        "w_fc": np.concatenate([t("L0_ffn_w_fc")] * 2, axis=0),
        "b_fc": a["L0_ffn_b_fc"].reshape(HC, 128).T,
        "w_proj": t("L0_ffn_w_proj"),
        "mixing": np.concatenate([
            np.array([[d % D < e for d in range(2 * D)] for e in EMBEDS for _ in RATIOS], dtype=f),
            np.array([[h < r * e for h in range(HID)] for e in EMBEDS for r in RATIOS], dtype=f),
            np.repeat(a["L0_ffn_alpha_e"], len(RATIOS))[:, None],
            np.tile(a["L0_ffn_alpha_r"], len(EMBEDS))[:, None]], axis=1),
    }
    arrays = {k: np.ascontiguousarray(v) for k, v in arrays.items()}
    nc = bacc.Bacc("TRN2", target_bir_lowering=False, num_devices=1)
    args = [nc.dram_tensor(f"in_{k}", v.shape, mybir.dt.from_np(v.dtype), kind="ExternalInput").ap()
            for k, v in arrays.items()]
    out = nc.dram_tensor("out_0", (B, T, D), mybir.dt.float32, kind="ExternalOutput").ap()
    lm_layer(nc, *args, out)
    r = run_bass_kernel_spmd(nc, [{f"in_{k}": v for k, v in arrays.items()}], core_ids=[0])
    return r.results[0]["out_0"]
```
